# Optimizing a Trainium2 kernel written in Bass

```python
import numpy as np
import jax
import jax.numpy as jnp

def _softmax(x, axis=-1):
    return jax.nn.softmax(x, axis=axis)

def _gelu(x):
    return jax.nn.gelu(x, approximate=True)

def _silu(x):
    return jax.nn.silu(x)

def _sigmoid(x):
    return jax.nn.sigmoid(x)

def _layernorm(x, axis=-1, eps=1e-05):
    m = jnp.mean(x, axis=axis, keepdims=True)
    v = jnp.var(x, axis=axis, keepdims=True)
    return (x - m) / jnp.sqrt(v + eps)

def _scatter_add(tgt, idx, src, axis=0):
    return tgt.at[idx].add(src)

def _segment_sum(src, seg, n):
    return jax.ops.segment_sum(src, seg, n)
kernel_name = 'mk_xattn_seq_d2_seqx_r4_6e86c1'

def setup_inputs(seed: int=0):
    np.random.seed(seed)
    _w = jnp.asarray

    def _rec_inputs():
        import jax
        import jax.numpy as jnp
        _rk = jax.random.key(seed)
        x = -0.0002928 + 1 * jax.random.normal(jax.random.fold_in(_rk, 1), (8, 256, 256), jnp.float32)
        _lenS = 256 - jax.random.randint(jax.random.fold_in(_rk, 7), (8,), 0, max(1, 256 // 4) + 1, jnp.int32)
        _lenS2 = 256 - jax.random.randint(jax.random.fold_in(_rk, 8), (8,), 0, max(1, 256 // 4) + 1, jnp.int32)
        _ctx_1024P = jax.random.normal(jax.random.fold_in(_rk, 11), (8, 16, 256), jnp.float32)
        _ctx_1024c = jax.random.dirichlet(jax.random.fold_in(_rk, 511), 0.3 * jnp.ones((16,), jnp.float32), (8, 256))
        _ctx_1024t = jnp.einsum('bsk,bkd->bsd', _ctx_1024c, _ctx_1024P)
        _ctx_1024t = _ctx_1024t * jax.lax.rsqrt(jnp.mean(jnp.square(_ctx_1024t)) + 1e-12) * 0.953939
        ctx_1024 = -1.39393e-06 + 0.999914 * (_ctx_1024t + 0.3 * jax.random.normal(jax.random.fold_in(_rk, 611), (8, 256, 256), jnp.float32))
        _validS = jnp.arange(256)[None, :] < _lenS[:, None]
        _validS2 = jnp.arange(256)[None, :] < _lenS2[:, None]
        _causal = jnp.tril(jnp.ones((256, 256), dtype=bool))
        mask_Bx1xSxS2_bk0 = jnp.logical_not(jnp.broadcast_to(_validS2[:, None, None, :], (8, 1, 256, 256)))
        mask_Bx1xSxS2_bf1 = jnp.ones((8, 1, 256, 256), dtype=bool)
        mask_BxSxS2_ik1 = jnp.where(jnp.broadcast_to(_validS2[:, None, :], (8, 256, 256)), 1, 0).astype(jnp.int32)
        return (x, ctx_1024, mask_Bx1xSxS2_bk0, mask_Bx1xSxS2_bf1, mask_BxSxS2_ik1)
    x, ctx_1024, mask_Bx1xSxS2_bk0, mask_Bx1xSxS2_bf1, mask_BxSxS2_ik1 = _rec_inputs()

    def _L0_xattn_setup():
        import jax, jax.numpy as jnp
        import numpy as np
        import math
        B, L, D, H, DFF = (2, 512, 256, 16, 1024)

        def _mha(xq, xkv, Wq, bq, Wk, bk, Wv, bv, Wo, bo, mask, h):
            b, lq, d = xq.shape
            dk = d // h
            q = (xq @ Wq + bq).reshape(b, lq, h, dk).transpose(0, 2, 1, 3)
            k = (xkv @ Wk + bk).reshape(b, -1, h, dk).transpose(0, 2, 1, 3)
            v = (xkv @ Wv + bv).reshape(b, -1, h, dk).transpose(0, 2, 1, 3)
            scores = jnp.einsum('bhqd,bhkd->bhqk', q, k) / jnp.sqrt(jnp.float32(dk))
            scores = jnp.where(mask, scores, jnp.float32(-1000000000.0))
            prob = jax.nn.softmax(scores, axis=-1)
            out = jnp.einsum('bhqk,bhkd->bhqd', prob, v)
            out = out.transpose(0, 2, 1, 3).reshape(b, lq, d)
            return out @ Wo + bo
        key = jax.random.key(seed)
        ks = jax.random.split(key, 16)
        s = 0.02
        inp = {'tgt': jax.random.normal(ks[0], (B, L, D), jnp.float32), 'encoder_out': jax.random.normal(ks[1], (B, L, D), jnp.float32), 'tgt_mask': jnp.broadcast_to(jnp.tril(jnp.ones((L, L), bool)), (B, 1, L, L)), 'src_tgt_mask': jnp.ones((B, 1, L, L), bool)}
        names = ['sWq', 'sWk', 'sWv', 'sWo', 'cWq', 'cWk', 'cWv', 'cWo']
        for i, n in enumerate(names):
            inp[n] = s * jax.random.normal(ks[2 + i], (D, D), jnp.float32)
            inp['sb' + n[2] if n[0] == 's' else 'cb' + n[2]] = jnp.zeros((D,), jnp.float32)
        inp['W1'] = s * jax.random.normal(ks[10], (D, DFF), jnp.float32)
        inp['b1'] = jnp.zeros((DFF,), jnp.float32)
        inp['W2'] = s * jax.random.normal(ks[11], (DFF, D), jnp.float32)
        inp['b2'] = jnp.zeros((D,), jnp.float32)
        return inp
    _L0_xattn_all = _L0_xattn_setup()
    _L0_xattn_in = {k: v for k, v in _L0_xattn_all.items() if k in ('sWq', 'sbq', 'sWk', 'sbk', 'sWv', 'sbv', 'sWo', 'sbo', 'cWq', 'cbq', 'cWk', 'cbk', 'cWv', 'cbv', 'cWo', 'cbo', 'W1', 'b1', 'W2', 'b2')}
    del _L0_xattn_all

    def _L1_xattn_setup():
        import jax, jax.numpy as jnp
        import numpy as np
        D_MODEL = 256
        N_HEAD = 16
        D_K = D_MODEL // N_HEAD
        LN_EPS = 1e-05

        def _split_heads(x, W):
            B, S, _ = x.shape
            y = jnp.einsum('bsd,ed->bse', x, W)
            return y.reshape(B, S, N_HEAD, D_K).transpose(0, 2, 1, 3)
        key = jax.random.key(seed)
        ks = jax.random.split(key, 9)
        B, S = (4, 512)
        scale = 1.0 / np.sqrt(D_MODEL)
        return {'query': jax.random.normal(ks[0], (B, S, D_MODEL), jnp.float32), 'key': jax.random.normal(ks[1], (B, S, D_MODEL), jnp.float32), 'value': jax.random.normal(ks[2], (B, S, D_MODEL), jnp.float32), 'mask': jax.random.randint(ks[3], (B, S, S), 0, 2, jnp.int32), 'W_Q': jax.random.normal(ks[4], (D_MODEL, D_MODEL), jnp.float32) * scale, 'W_K': jax.random.normal(ks[5], (D_MODEL, D_MODEL), jnp.float32) * scale, 'W_V': jax.random.normal(ks[6], (D_MODEL, D_MODEL), jnp.float32) * scale, 'W_O': jax.random.normal(ks[7], (D_MODEL, D_MODEL), jnp.float32) * scale, 'gamma': jnp.ones((D_MODEL,), jnp.float32), 'beta': jnp.zeros((D_MODEL,), jnp.float32)}
    _L1_xattn_all = _L1_xattn_setup()
    _L1_xattn_in = {k: v for k, v in _L1_xattn_all.items() if k in ('W_Q', 'W_K', 'W_V', 'W_O', 'gamma', 'beta')}
    del _L1_xattn_all
    return {'x': x, 'ctx_1024': ctx_1024, 'mask_Bx1xSxS2_bk0': mask_Bx1xSxS2_bk0, 'mask_Bx1xSxS2_bf1': mask_Bx1xSxS2_bf1, 'mask_BxSxS2_ik1': mask_BxSxS2_ik1, 'L0_xattn_sWq': _L0_xattn_in['sWq'], 'L0_xattn_sbq': _L0_xattn_in['sbq'], 'L0_xattn_sWk': _L0_xattn_in['sWk'], 'L0_xattn_sbk': _L0_xattn_in['sbk'], 'L0_xattn_sWv': _L0_xattn_in['sWv'], 'L0_xattn_sbv': _L0_xattn_in['sbv'], 'L0_xattn_sWo': _L0_xattn_in['sWo'], 'L0_xattn_sbo': _L0_xattn_in['sbo'], 'L0_xattn_cWq': _L0_xattn_in['cWq'], 'L0_xattn_cbq': _L0_xattn_in['cbq'], 'L0_xattn_cWk': _L0_xattn_in['cWk'], 'L0_xattn_cbk': _L0_xattn_in['cbk'], 'L0_xattn_cWv': _L0_xattn_in['cWv'], 'L0_xattn_cbv': _L0_xattn_in['cbv'], 'L0_xattn_cWo': _L0_xattn_in['cWo'], 'L0_xattn_cbo': _L0_xattn_in['cbo'], 'L0_xattn_W1': _L0_xattn_in['W1'], 'L0_xattn_b1': _L0_xattn_in['b1'], 'L0_xattn_W2': _L0_xattn_in['W2'], 'L0_xattn_b2': _L0_xattn_in['b2'], 'L1_xattn_W_Q': _L1_xattn_in['W_Q'], 'L1_xattn_W_K': _L1_xattn_in['W_K'], 'L1_xattn_W_V': _L1_xattn_in['W_V'], 'L1_xattn_W_O': _L1_xattn_in['W_O'], 'L1_xattn_gamma': _L1_xattn_in['gamma'], 'L1_xattn_beta': _L1_xattn_in['beta']}

def reference(x, ctx_1024, mask_Bx1xSxS2_bk0, mask_Bx1xSxS2_bf1, mask_BxSxS2_ik1, L0_xattn_sWq, L0_xattn_sbq, L0_xattn_sWk, L0_xattn_sbk, L0_xattn_sWv, L0_xattn_sbv, L0_xattn_sWo, L0_xattn_sbo, L0_xattn_cWq, L0_xattn_cbq, L0_xattn_cWk, L0_xattn_cbk, L0_xattn_cWv, L0_xattn_cbv, L0_xattn_cWo, L0_xattn_cbo, L0_xattn_W1, L0_xattn_b1, L0_xattn_W2, L0_xattn_b2, L1_xattn_W_Q, L1_xattn_W_K, L1_xattn_W_V, L1_xattn_W_O, L1_xattn_gamma, L1_xattn_beta):
    import jax
    import jax.numpy as jnp

    def _L0_xattn_ref(tgt, encoder_out, tgt_mask, src_tgt_mask, sWq, sbq, sWk, sbk, sWv, sbv, sWo, sbo, cWq, cbq, cWk, cbk, cWv, cbv, cWo, cbo, W1, b1, W2, b2):
        import jax, jax.numpy as jnp
        import numpy as np
        import math
        B, L, D, H, DFF = (2, 512, 256, 16, 1024)

        def _mha(xq, xkv, Wq, bq, Wk, bk, Wv, bv, Wo, bo, mask, h):
            b, lq, d = xq.shape
            dk = d // h
            q = (xq @ Wq + bq).reshape(b, lq, h, dk).transpose(0, 2, 1, 3)
            k = (xkv @ Wk + bk).reshape(b, -1, h, dk).transpose(0, 2, 1, 3)
            v = (xkv @ Wv + bv).reshape(b, -1, h, dk).transpose(0, 2, 1, 3)
            scores = jnp.einsum('bhqd,bhkd->bhqk', q, k) / jnp.sqrt(jnp.float32(dk))
            scores = jnp.where(mask, scores, jnp.float32(-1000000000.0))
            prob = jax.nn.softmax(scores, axis=-1)
            out = jnp.einsum('bhqk,bhkd->bhqd', prob, v)
            out = out.transpose(0, 2, 1, 3).reshape(b, lq, d)
            return out @ Wo + bo
        x = tgt + _mha(tgt, tgt, sWq, sbq, sWk, sbk, sWv, sbv, sWo, sbo, tgt_mask, H)
        x = x + _mha(x, encoder_out, cWq, cbq, cWk, cbk, cWv, cbv, cWo, cbo, src_tgt_mask, H)
        x = x + (jax.nn.relu(x @ W1 + b1) @ W2 + b2)
        return x

    def _L1_xattn_ref(query, key, value, mask, W_Q, W_K, W_V, W_O, gamma, beta):
        import jax, jax.numpy as jnp
        import numpy as np
        D_MODEL = 256
        N_HEAD = 16
        D_K = D_MODEL // N_HEAD
        LN_EPS = 1e-05

        def _split_heads(x, W):
            B, S, _ = x.shape
            y = jnp.einsum('bsd,ed->bse', x, W)
            return y.reshape(B, S, N_HEAD, D_K).transpose(0, 2, 1, 3)
        residual = query
        B, S, _ = query.shape
        q = _split_heads(query, W_Q)
        k = _split_heads(key, W_K)
        v = _split_heads(value, W_V)
        scores = jnp.einsum('bhqd,bhkd->bhqk', q, k) / np.sqrt(D_K)
        scores = jnp.where(mask[:, None, :, :] == 1, jnp.float32(-1000000000.0), scores)
        p = jax.nn.softmax(scores, axis=-1)
        ctx = jnp.einsum('bhqk,bhkd->bhqd', p, v)
        concat = ctx.transpose(0, 2, 1, 3).reshape(B, S, D_MODEL)
        out = jnp.einsum('bsd,ed->bse', concat, W_O) + residual
        mu = jnp.mean(out, axis=-1, keepdims=True)
        var = jnp.mean((out - mu) ** 2, axis=-1, keepdims=True)
        return (out - mu) * jax.lax.rsqrt(var + LN_EPS) * gamma + beta
    x = _L0_xattn_ref(x, ctx_1024, mask_Bx1xSxS2_bk0, mask_Bx1xSxS2_bf1, L0_xattn_sWq, L0_xattn_sbq, L0_xattn_sWk, L0_xattn_sbk, L0_xattn_sWv, L0_xattn_sbv, L0_xattn_sWo, L0_xattn_sbo, L0_xattn_cWq, L0_xattn_cbq, L0_xattn_cWk, L0_xattn_cbk, L0_xattn_cWv, L0_xattn_cbv, L0_xattn_cWo, L0_xattn_cbo, L0_xattn_W1, L0_xattn_b1, L0_xattn_W2, L0_xattn_b2)
    x = _L1_xattn_ref(x, ctx_1024, ctx_1024, mask_BxSxS2_ik1, L1_xattn_W_Q, L1_xattn_W_K, L1_xattn_W_V, L1_xattn_W_O, L1_xattn_gamma, L1_xattn_beta)
    return x

_drawn_inputs = setup_inputs


def setup_inputs(seed=0):
    import zlib

    import numpy as np

    out = dict(_drawn_inputs(seed))
    spreads = {'L0_xattn_sbq': (0.0, 0.8),
     'L0_xattn_sbk': (0.0, 0.8),
     'L0_xattn_sbv': (0.0, 0.284),
     'L0_xattn_sbo': (0.0, 0.1),
     'L0_xattn_cbq': (0.0, 0.8),
     'L0_xattn_cbk': (0.0, 0.8),
     'L0_xattn_cbv': (0.0, 0.291),
     'L0_xattn_cbo': (0.0, 0.1),
     'L0_xattn_b1': (0.0, 0.1),
     'L0_xattn_b2': (0.0, 0.1),
     'L1_xattn_gamma': (1.0, 0.2),
     'L1_xattn_beta': (0.0, 0.1)}
    factors = {'L0_xattn_sWq': 8.0,
     'L0_xattn_sWk': 8.0,
     'L0_xattn_sWv': 2.746,
     'L0_xattn_cWq': 8.0,
     'L0_xattn_cWk': 8.0}
    for name, (base, spread) in spreads.items():
        noise = np.random.default_rng([zlib.crc32(name.encode()), seed]).standard_normal(out[name].shape)
        drawn = base * np.exp(spread * noise) if base else spread * noise
        out[name] = jnp.asarray(drawn.astype(out[name].dtype))
    for name, factor in factors.items():
        out[name] = (out[name] * factor).astype(out[name].dtype)
    return out
```

```python
from contextlib import ExitStack

import numpy as np

import concourse.bass as bass
from concourse import mybir

P = 128
BATCH, TOKENS, WIDTH, HEADS, HIDDEN = 8, 256, 256, 16, 1024
HEAD = WIDTH // HEADS
STAGES = 3
UNITS = STAGES * BATCH
HALVES = WIDTH // P
PAIRS = HEADS // 2
PARTS = 3
HALF_ROWS = PARTS * HEAD
STACK_ROWS = 2 * HALF_ROWS
MAX_ROWS = STACK_ROWS + 4
GROUPS = 4
SHIFT = 6
SCALE = HEAD ** -0.5
BIG = 1.0e30
HUGE = 3.0e38
EPS = 1e-5
NEWTON = 3
NEWTON_OPS = 4 * NEWTON

F32 = mybir.dt.float32
F32R = mybir.dt.float32r
BF16 = mybir.dt.bfloat16
U8 = mybir.dt.uint8
I32 = mybir.dt.int32
ALU = mybir.AluOpType
ACT = mybir.ActivationFunctionType


class Unit:

    def __init__(self, n, n_min, p):
        self.n, self.p = n, p
        self.u = n * 2 + p
        self.u_min = 2 * n_min + p
        self.stage = self.u_min // BATCH
        self.valid = 0 <= self.u_min < UNITS
        self.batch = self.u - BATCH * self.stage


def reached(eng, sem, unit, per, count, back=0):
    least = per * (unit.u_min - back) + count
    if unit.u_min - back >= 0 and least > 0:
        eng.wait_ge(sem, unit.u * per + (count - per * back))


def landed(eng, sem, unit, per, back=0):
    if unit.u_min - 2 * back >= 0:
        eng.wait_ge(sem[unit.p], (unit.n - back + 1) * per)


def apart(eng, sem):
    eng.sem_inc(sem, 1)


def steps():
    def work(i):
        out = []
        for par in range(2):
            for ahead in (2, 1, 0, -1, -2):
                u = 2 * i + par + ahead
                has_stage = ahead in (2, -2) and 0 <= u < UNITS
                out.append((u // BATCH if has_stage else 0 <= u < UNITS, u >= 2))
        return out

    runs = []
    for i in range(-1, UNITS // 2 + 1):
        if runs and work(i) == work(runs[-1][0]):
            runs[-1][1] = i + 1
        else:
            runs.append([i, i + 1])
    return runs


def run_steps(eng, body):
    for first, end in steps():
        def two_steps(i):
            for par in range(2):
                def at(ahead):
                    o = par + ahead
                    return Unit(i + o // 2, first + o // 2, o % 2)
                body(at(2), at(1), at(0), at(-1), at(-2))
        if end - first == 1:
            two_steps(first)
        else:
            with eng.Fori(first, end) as i:
                two_steps(i)


def head_of(slot):
    return slot // 2 + (slot % 2) * PAIRS


def build(nc, t):
    ctx = ExitStack()
    with ctx:
        def sb(name, shape, dt=F32):
            return ctx.enter_context(nc.sbuf_tensor(name, shape, dt))

        def sem(name):
            return ctx.enter_context(nc.semaphore(name))

        def sem2(name):
            return [sem(f"{name}{p}") for p in range(2)]

        def two(name, shape, dt=F32):
            return [sb(f"{name}{p}", shape, dt) for p in range(2)]

        w = [{c: sb(f"w{c}{s}", [P, HALVES, WIDTH]) for c in "qkvo"} for s in range(STAGES)]
        w1 = sb("w1", [P, HALVES, HIDDEN])
        w2 = sb("w2", [P, HIDDEN // P, WIDTH])
        cols = sb("cols", [P, 2 * 3 * HALVES])
        zero_col = sb("zero_col", [P, HALVES])
        b1 = sb("b1", [P, HIDDEN // P])
        b2 = sb("b2", [P, HALVES])
        bv = sb("bv", [P, STAGES, WIDTH])
        gamma = sb("gamma", [P, WIDTH])
        beta = sb("beta", [P, WIDTH])
        ident = sb("ident", [P, P])
        ones = sb("ones", [P, P], BF16)
        max_sign = sb("max_sign", [P, HEADS])
        xq = two("xq", [P, HALVES, TOKENS])
        xkv = two("xkv", [P, HALVES, TOKENS])
        raw32 = two("raw32", [P, 2, HALVES, TOKENS], I32)
        raw_words = [r[:, :, :, 0:TOKENS // 4] for r in raw32]
        raw8 = [r[:].bitcast(U8)[:, :, :, 0:TOKENS] for r in raw32]
        allow = sb("allow", [P, 2, HALVES, TOKENS], BF16)
        some = sb("some", [P, TOKENS], BF16)
        none = sb("none", [P, TOKENS], BF16)
        some_big = sb("some_big", [P, HALVES])
        bias = two("bias", [P, HALVES, TOKENS], BF16)
        seen = sb("seen", [P, HALVES, TOKENS], BF16)
        ident16 = sb("ident16", [P, P], BF16)
        bias_a = two("bias_a", [P, HALVES, TOKENS], BF16)
        v_a = two("v_a", [P, HALVES, WIDTH])
        qf = sb("qf", [P, HALVES, TOKENS])
        kf = sb("kf", [P, HALVES, TOKENS])
        q_parts = sb("q_parts", [P, 2, HALVES, TOKENS], F32R)
        k_parts = sb("k_parts", [P, 2, HALVES, TOKENS], F32R)
        q_stack = two("q_stack", [P, PAIRS, TOKENS], F32R)
        k_stack = two("k_stack", [P, HEADS, TOKENS], F32R)
        mx = two("mx", [P, HALVES, HEADS])
        m_parts = sb("m_parts", [HEADS, 2, TOKENS], F32R)
        probs = sb("probs", [P, GROUPS, 4, HALVES * TOKENS])
        bias_c = two("bias_c", [P, HALVES * TOKENS], BF16)
        v_c = two("v_c", [P, HALVES, HEADS, 32])
        sums = two("sums", [P, GROUPS, TOKENS])
        rcp = sb("rcp", [P, HALVES, HEADS])
        ctx_tok = sb("ctx_tok", [P, HALVES, WIDTH])
        ctx_feat = sb("ctx_feat", [P, HALVES, TOKENS])
        res = two("res", [P, HALVES, TOKENS])
        hid = sb("hid", [P, HIDDEN // P, TOKENS])
        stats = sb("stats", [P, HALVES, 6])
        aggr = sb("aggr", [P, HALVES, 2])
        var_eps = sb("var_eps", [P, HALVES])
        guess_bits = sb("guess_bits", [P, HALVES], I32)
        rstd = sb("rstd", [P, 2, HALVES])
        newton = sb("newton", [P, 3, HALVES])

        def bank(name):
            return ctx.enter_context(nc.psum_tensor(name, [P, 512], F32))

        ps_a = bank("ps_a")
        ps_s = [bank(f"ps_s{i}") for i in range(2)]
        ps_t = [bank(f"ps_t{i}") for i in range(2)]
        ps_o = bank("ps_o")
        ps_d = [bank(f"ps_d{i}") for i in range(2)]

        x_wait = nc.dram_tensor("x_wait", [UNITS, WIDTH, TOKENS], F32).ap()
        q_img = nc.dram_tensor("q_img", [2, 2, PARTS, HEAD, PAIRS, TOKENS], F32).ap()
        k_img = nc.dram_tensor("k_img", [2, 2, PARTS, HEAD, PAIRS, TOKENS], F32).ap()
        m_img = nc.dram_tensor("m_img", [2, 2, 2, PAIRS, TOKENS], F32).ap()

        const_in, const_set, const_set2 = sem("const_in"), sem("const_set"), sem("const_set2")
        in_ready = sem2("in_ready")
        img_written = sem2("img_written")
        stack_ready = [sem2("stack_ready_lo"), sem2("stack_ready_hi")]
        m_written, m_ready = sem2("m_written"), sem2("m_ready")
        res_ready, stored = sem2("res_ready"), sem2("stored")
        count_mm, q_mm, k_mm, v_mm = sem("count_mm"), sem("q_mm"), sem("k_mm"), sem("v_mm")
        m_turned, s_mm, t_mm, pv_mm = sem("m_turned"), sem("s_mm"), sem("t_mm"), sem("pv_mm")
        sums_turned, ctx_turned, o_mm = sem("sums_turned"), sem("ctx_turned"), sem("o_mm")
        hid_mm, ffn_mm = sem("hid_mm"), sem("ffn_mm")
        allow_set, some_set, none_set, big_set = sem("allow_set"), sem("some_set"), sem("none_set"), sem("big_set")
        bias_a_set, bias_set, q_out, v_out = sem("bias_a_set"), sem("bias_set"), sem("q_out"), sem("v_out")
        max_set, m_lo, rcp_set, normed = sem("max_set"), sem("m_lo"), sem("rcp_set"), sem("normed")
        y_set, y_set2, z_set, handed_v = sem("y_set"), sem("y_set2"), sem("z_set"), sem("handed_v")
        d_done, ln_stats, ln_aggr, ln_gamma, ln_out = (
            sem("d_done"), sem("ln_stats"), sem("ln_aggr"), sem("ln_gamma"), sem("ln_out"))
        k_out, q_hi, k_hi, m_hi, exp_done = sem("k_out"), sem("q_hi"), sem("k_hi"), sem("m_hi"), sem("exp_done")
        sums_out, ctx_out, handed, relu_done = sem("sums_out"), sem("ctx_out"), sem("handed"), sem("relu_done")
        q_lo, k_lo, rstd_set = sem("q_lo"), sem("k_lo"), sem("rstd_set")
        dve_passed, pool_passed, sp_passed = sem("dve_passed"), sem("pool_passed"), sem("sp_passed")
        guess, seen_set = sem("guess"), sem("seen_set")

        CONSTS = 4 * STAGES + 2 + 1 + 2 + 2 + 2 + 1 + 1

        def col(stage, which):
            if stage == 2:
                return zero_col
            o = (3 * stage + "qko".index(which)) * HALVES
            return cols[:, o:o + HALVES]

        def feat(ap):
            return ap.rearrange("(t p) q -> p t q", p=P)

        block = ctx.enter_context(nc.Block())

        @block.sync
        def _(sp):
            for s in range(STAGES):
                for c in "qkvo":
                    sp.dma_start(w[s][c][:], feat(t[f"w{c}{s}"])).then_inc(const_in, 16)
            sp.dma_start(w1[:], feat(t["w1"])).then_inc(const_in, 16)
            sp.dma_start(w2[:], feat(t["w2"])).then_inc(const_in, 16)
            sp.dma_start(cols[:], t["cols"]).then_inc(const_in, 16)
            sp.dma_start(b1[:], t["b1"]).then_inc(const_in, 16)
            sp.dma_start(b2[:], t["b2"]).then_inc(const_in, 16)
            for s in range(2):
                sp.dma_start(bv[:, s, :], t[f"bv{s}"].broadcast_to([P, WIDTH])).then_inc(const_in, 16)
            sp.dma_start(gamma[:], t["gamma"].broadcast_to([P, WIDTH])).then_inc(const_in, 16)
            sp.dma_start(beta[:], t["beta"].broadcast_to([P, WIDTH])).then_inc(const_in, 16)
            sp.dma_start(ident[:], t["ident"]).then_inc(const_in, 16)
            sp.dma_start(max_sign[STACK_ROWS:P, :], t["max_sign"]).then_inc(const_in, 16)

            def load(a):
                reached(sp, v_mm, a, 1, 1, back=2)
                apart(sp, sp_passed)
                reached(sp, allow_set, a, 2, 2, back=2)
                apart(sp, sp_passed)
                x_in = t["x"][a.batch] if a.stage == 0 else x_wait[a.u]
                if a.stage > 0:
                    landed(sp, stored, a, 16, back=BATCH // 2)
                    apart(sp, sp_passed)
                sp.dma_start(xq[a.p][:], feat(x_in)).then_inc(in_ready[a.p], 16)
                kv_in = t["x"][a.batch] if a.stage == 0 else t["ctx"][a.batch]
                sp.dma_start(xkv[a.p][:], feat(kv_in)).then_inc(in_ready[a.p], 16)
                raw = raw32 if a.stage == 2 else raw_words
                for o in range(2):
                    sp.dma_start(raw[a.p][:, o], t[f"mask{a.stage}"][a.batch, o].rearrange("(t p) q -> p t q", p=P)
                                 ).then_inc(in_ready[a.p], 16)

            def write_stacks(a):
                landed(sp, stack_ready[0], a, 48, back=1)
                apart(sp, sp_passed)
                landed(sp, stack_ready[1], a, 48, back=1)
                apart(sp, sp_passed)
                for parts, img, order, done in ((q_parts, q_img, (0, 0, 1), q_lo), (k_parts, k_img, (0, 1, 0), k_lo)):
                    reached(sp, done, a, 1, 1)
                    apart(sp, sp_passed)
                    for c, part in enumerate(order):
                        dst = img[a.p, :, c].rearrange("t r j q -> j r t q")
                        for t_ in range(HALVES):
                            sp.dma_start(dst[:, :, t_, :], parts[:, part, t_, :].bitcast(F32)).then_inc(img_written[a.p], 16)

            def read_stacks(a, g):
                landed(sp, img_written, a, 16 * 12)
                apart(sp, sp_passed)
                reached(sp, t_mm, a, HEADS, 8 * g + 8, back=2)
                apart(sp, sp_passed)
                j = slice(4 * g, 4 * g + 4)
                sem_ = stack_ready[g][a.p]
                sp.dma_start(q_stack[a.p][0:STACK_ROWS, j, :].bitcast(F32),
                             q_img[a.p].rearrange("t c r j q -> (t c r) j q")[:, j, :]).then_inc(sem_, 16)
                for half in range(2):
                    sp.dma_start(k_stack[a.p][half * HALF_ROWS:(half + 1) * HALF_ROWS,
                                              half * PAIRS + 4 * g:half * PAIRS + 4 * g + 4, :].bitcast(F32),
                                 k_img[a.p, half].rearrange("c r j q -> (c r) j q")[:, j, :]).then_inc(sem_, 16)

            def pass_max(c):
                landed(sp, m_ready, c, 16, back=1)
                apart(sp, sp_passed)
                reached(sp, m_lo, c, 1, 1)
                apart(sp, sp_passed)
                for half in range(2):
                    sp.dma_start(m_img[c.p, half].rearrange("c j q -> j c q"),
                                 m_parts[half * PAIRS:(half + 1) * PAIRS].bitcast(F32)).then_inc(m_written[c.p], 16)
                landed(sp, m_written, c, 32)
                apart(sp, sp_passed)
                reached(sp, t_mm, c, HEADS, HEADS, back=2)
                apart(sp, sp_passed)
                sp.dma_start(q_stack[c.p][STACK_ROWS:MAX_ROWS].bitcast(F32),
                             m_img[c.p].rearrange("t c j q -> (t c) j q")).then_inc(m_ready[c.p], 16)

            def load_res(d):
                landed(sp, stored, d, 16, back=1)
                apart(sp, sp_passed)
                x_in = t["x"][d.batch] if d.stage == 0 else x_wait[d.u]
                sp.dma_start(res[d.p][:], feat(x_in)).then_inc(res_ready[d.p], 16)

            def store(d):
                if d.stage == 2:
                    eng_out = t["out"][d.batch].rearrange("(t p) e -> p t e", p=P)
                    sp.wait_ge(ln_out, d.batch + 1)
                    apart(sp, sp_passed)
                    sp.dma_start(eng_out, res[d.p][:]).then_inc(stored[d.p], 16)
                else:
                    reached(sp, d_done, d, 1, 1)
                    apart(sp, sp_passed)
                    sp.dma_start(feat(x_wait[d.u + BATCH]), res[d.p][:]
                                 ).then_inc(stored[d.p], 16)

            def step(a, b, c, c_before, d):
                if a.valid:
                    load(a)
                if d.valid:
                    load_res(d)
                if c.valid:
                    pass_max(c)
                if b.valid:
                    read_stacks(b, 1)
                if a.valid:
                    write_stacks(a)
                if d.valid:
                    store(d)
                if a.valid:
                    read_stacks(a, 0)

            run_steps(sp, step)
            for p in range(2):
                sp.wait_ge(stored[p], 16 * UNITS // 2)

        @block.tensor
        def _(pe):
            mm = nc.tensor.matmul

            def count_keys(a):
                reached(pe, allow_set, a, 2, 1)
                reached(pe, v_out, a, 1, 1, back=1)
                reached(pe, m_lo, a, 1, 1, back=2)
                for k in range(HALVES):
                    mm(ps_a[:, 0:TOKENS], ones[:], allow[:, 0, k, :], start=(k == 0), stop=(k == HALVES - 1))
                for q in range(HALVES):
                    for k in range(HALVES):
                        last = mm(ps_a[:, TOKENS + 2 * q:TOKENS + 2 * q + 2], allow[:, 0, k, q * P:(q + 1) * P],
                                  ones[:, 0:2], start=(k == 0), stop=(k == HALVES - 1))
                last.then_inc(count_mm, 1)

            def project(weights, moving, done):
                for m in range(HALVES):
                    for k in range(HALVES):
                        last = mm(ps_a[:, m * TOKENS:(m + 1) * TOKENS], weights[:, k, m * P:(m + 1) * P],
                                  moving[:, k, :], start=(k == 0), stop=(k == HALVES - 1))
                last.then_inc(done, 1)

            def project_q(a):
                landed(pe, in_ready, a, 64)
                reached(pe, some_set, a, 1, 1)
                reached(pe, big_set, a, 1, 1)
                project(w[a.stage]["q"], xq[a.p], q_mm)

            def project_k(a):
                reached(pe, q_out, a, 2, 2)
                project(w[a.stage]["k"], xkv[a.p], k_mm)

            def project_v(a):
                reached(pe, k_out, a, 2, 2)
                for m in range(HALVES):
                    for k in range(HALVES):
                        last = mm(ps_a[:, m * WIDTH:(m + 1) * WIDTH], xkv[a.p][:, k, m * P:(m + 1) * P],
                                  w[a.stage]["v"][:, k, :], start=(k == 0), stop=(k == HALVES - 1))
                last.then_inc(v_mm, 1)

            def scores(b, slot):
                if slot % 8 == 0:
                    landed(pe, stack_ready[slot // 8], b, 48)
                reached(pe, max_set, b, 2 * HEADS, 2 * slot - 2)
                if slot < 2:
                    reached(pe, max_set, b, 2 * HEADS, 2 * HEADS + 2 * slot - 2, back=1)
                for q in range(HALVES):
                    last = mm(ps_s[slot % 2][:, q * TOKENS:(q + 1) * TOKENS],
                              q_stack[b.p][0:STACK_ROWS, slot // 2, q * P:(q + 1) * P],
                              k_stack[b.p][0:STACK_ROWS, head_of(slot), :], start=True, stop=True)
                last.then_inc(s_mm, 1)

            def turn_max(c):
                reached(pe, max_set, c, 2 * HEADS, 2 * HEADS)
                reached(pe, v_out, c, 1, 1)
                if c.u_min + 1 < UNITS:
                    reached(pe, v_out, c, 1, 2)
                for q in range(HALVES):
                    last = nc.tensor.transpose(ps_a[0:HEADS, q * P:(q + 1) * P], mx[c.p][:, q, :], ident[:])
                last.then_inc(m_turned, 1)

            def scores_less_max(c, slot):
                if slot == 0:
                    landed(pe, m_ready, c, 16)
                    reached(pe, handed, c, 2, 2)
                reached(pe, exp_done, c, HEADS, slot - 1)
                if slot < 1:
                    reached(pe, exp_done, c, HEADS, HEADS + slot - 1, back=1)
                mm(ps_t[slot % 2][:], ident16[:], bias_c[c.p][:], start=True, stop=False, skip_group_check=True)
                for k in range(HALVES):
                    last = mm(ps_t[slot % 2][:, k * TOKENS:(k + 1) * TOKENS],
                              k_stack[c.p][0:MAX_ROWS, head_of(slot), k * P:(k + 1) * P],
                              q_stack[c.p][0:MAX_ROWS, slot // 2, :], start=False, stop=(k == HALVES - 1),
                              skip_group_check=True)
                last.then_inc(t_mm, 1)

            def weigh_values(c, g):
                reached(pe, exp_done, c, HEADS, 4 * g + 4)
                if g == 0:
                    reached(pe, handed, c, 2, 2)
                if g % 2 == 0:
                    reached(pe, sums_out, c, 2, g // 2)
                for k in range(HALVES):
                    for j in range(4):
                        last = mm(ps_o[32 * j:32 * j + 32, (g % 2) * TOKENS:(g % 2 + 1) * TOKENS],
                                  v_c[c.p][:, k, 4 * g + j, :], probs[:, g, j, k * TOKENS:(k + 1) * TOKENS],
                                  start=(k == 0), stop=(k == HALVES - 1), tile_position=(0, 32 * j))
                last.then_inc(pv_mm, 1)

            def turn_sums(d):
                reached(pe, sums_out, d, 2, 2)
                reached(pe, d_done, d, 1, 1, back=1)
                for q in range(HALVES):
                    for g in range(GROUPS):
                        last = nc.tensor.transpose(ps_d[q][:, g * P:(g + 1) * P],
                                                   sums[d.p][:, g, q * P:(q + 1) * P], ident[:])
                last.then_inc(sums_turned, 1)

            def turn_ctx(d):
                reached(pe, normed, d, 2, 2)
                for f in range(HALVES):
                    for q in range(HALVES):
                        last = nc.tensor.transpose(ps_d[0][:, f * TOKENS + q * P:f * TOKENS + (q + 1) * P],
                                                   ctx_tok[:, q, f * P:(f + 1) * P], ident[:])
                last.then_inc(ctx_turned, 1)

            def project_out(d):
                reached(pe, ctx_out, d, 1, 1)
                wo = w[d.stage]["o"]
                if d.stage < 2:
                    for m in range(HALVES):
                        for k in range(HALVES):
                            last = mm(ps_d[1][:, m * TOKENS:(m + 1) * TOKENS], wo[:, k, m * P:(m + 1) * P],
                                      ctx_feat[:, k, :], start=(k == 0), stop=(k == HALVES - 1))
                else:
                    landed(pe, res_ready, d, 16)
                    for m in range(HALVES):
                        for k in range(HALVES):
                            mm(ps_d[1][:, m * WIDTH:(m + 1) * WIDTH], ctx_feat[:, k, m * P:(m + 1) * P],
                               wo[:, k, :], start=(k == 0), stop=False, skip_group_check=True)
                        for k in range(HALVES):
                            last = mm(ps_d[1][:, m * WIDTH + k * P:m * WIDTH + (k + 1) * P],
                                      res[d.p][:, k, m * P:(m + 1) * P], ident[:], start=False,
                                      stop=(k == HALVES - 1), skip_group_check=True)
                last.then_inc(o_mm, 1)

            def hidden(d, m2):
                if m2 == 0:
                    pe.wait_ge(y_set, (d.batch + 1) * 2)
                elif m2 > 1:
                    pe.wait_ge(relu_done, d.batch * 8 + 2 * (m2 - 1))
                for m in range(2):
                    for k in range(HALVES):
                        o = (2 * m2 + m) * P
                        last = mm(ps_d[m2 % 2][:, m * TOKENS:(m + 1) * TOKENS], w1[:, k, o:o + P],
                                  res[d.p][:, k, :], start=(k == 0), stop=(k == HALVES - 1))
                last.then_inc(hid_mm, 1)

            def ffn_out(d):
                pe.wait_ge(relu_done, (d.batch + 1) * 8)
                for m in range(HALVES):
                    for k in range(HIDDEN // P):
                        last = mm(ps_d[0][:, m * TOKENS:(m + 1) * TOKENS], w2[:, k, m * P:(m + 1) * P],
                                  hid[:, k, :], start=(k == 0), stop=(k == HIDDEN // P - 1))
                last.then_inc(ffn_mm, 1)

            def step(a, b, c, c_before, d):
                for k in range(HEADS):
                    if k == 0 and d.valid:
                        turn_sums(d)
                    if k == 1 and c.valid:
                        turn_max(c)
                    if a.valid:
                        if k == 2:
                            count_keys(a)
                        if k == 4:
                            project_q(a)
                        if k == 6:
                            project_k(a)
                        if k == 8:
                            project_v(a)
                    if b.valid:
                        scores(b, k)
                    if k < SHIFT:
                        if c_before.valid:
                            scores_less_max(c_before, k + HEADS - SHIFT)
                    elif c.valid:
                        scores_less_max(c, k - SHIFT)
                    if c_before.valid and k in (2, 6, 10):
                        weigh_values(c_before, k // 4 + 1)
                    if c.valid and k == 14:
                        weigh_values(c, 0)
                    if d.valid:
                        if k == 3:
                            turn_ctx(d)
                        if k == 6:
                            project_out(d)
                        if d.stage == 1 and k in (9, 10, 12, 13):
                            hidden(d, (9, 10, 12, 13).index(k))
                        if d.stage == 1 and k == 15:
                            ffn_out(d)

            pe.wait_ge(const_in, 16 * CONSTS)
            pe.wait_ge(const_set, 5)
            pe.wait_ge(const_set2, 5)
            run_steps(pe, step)

        @block.vector
        def _(dve):
            nc.vector.memset(zero_col[:], 0.0).then_inc(const_set, 1)
            nc.vector.memset(ones[:], 1.0).then_inc(const_set, 1)
            nc.vector.memset(bv[:, 2, :], 0.0).then_inc(const_set, 1)
            for p in range(2):
                nc.vector.memset(v_c[p][:, :, :, HEAD:32], 1.0).then_inc(const_set, 1)
            for p in range(2):
                nc.vector.memset(k_stack[p][0:STACK_ROWS].bitcast(F32), 0.0).then_inc(const_set2, 1)
            dve.wait_ge(const_in, 16 * CONSTS)
            for p in range(2):
                nc.vector.tensor_copy(k_stack[p][STACK_ROWS:P],
                                      max_sign[STACK_ROWS:P, :, None].broadcast_to([P - STACK_ROWS, HEADS, TOKENS])
                                      ).then_inc(const_set2, 1)
            nc.vector.tensor_copy(ident16[:], ident[:]).then_inc(const_set2, 1)
            dve.wait_ge(const_set, 5)

            def set_allow(a):
                landed(dve, in_ready, a, 64)
                reached(dve, count_mm, a, 1, 1, back=1)
                reached(dve, bias_a_set, a, 1, 1, back=1)
                reached(dve, bias_set, a, 2, 2, back=1)
                raw, blocked = (raw32, 1.0) if a.stage == 2 else (raw8, 0.0)
                for o in range(2):
                    nc.vector.tensor_scalar(allow[:, o], raw[a.p][:, o], blocked, None,
                                            ALU.not_equal).then_inc(allow_set, 1)

            def set_masks(a):
                reached(dve, count_mm, a, 1, 1)
                reached(dve, q_out, a, 2, 2, back=1)
                reached(dve, bias_a_set, a, 1, 1, back=1)
                nc.vector.tensor_scalar(some[:], ps_a[:, 0:TOKENS], 1.0, None, ALU.min).then_inc(some_set, 1)
                nc.vector.tensor_scalar(
                    some_big[:], ps_a[:, TOKENS:TOKENS + 4].rearrange("p (q two) -> p q two", two=2)[:, :, 0],
                    1.0, BIG, ALU.min, ALU.mult).then_inc(big_set, 1)
                reached(dve, some_set, a, 1, 1)
                nc.vector.tensor_scalar(none[:], some[:], -1.0, 1.0, ALU.mult, ALU.add).then_inc(none_set, 1)
                reached(dve, big_set, a, 1, 1)
                reached(dve, allow_set, a, 2, 2)
                reached(dve, max_set, a, 2 * HEADS, 2 * HEADS, back=2)
                for q in range(HALVES):
                    nc.vector.tensor_scalar(bias[a.p][:, q], allow[:, 1, q], some_big[:, q:q + 1],
                                            some_big[:, q:q + 1], ALU.mult, ALU.subtract).then_inc(bias_set, 1)
                reached(dve, none_set, a, 1, 1)
                reached(dve, handed, a, 2, 2, back=2)
                nc.vector.tensor_tensor(seen[:], allow[:, 0], none[:, None, :].broadcast_to([P, HALVES, TOKENS]),
                                        ALU.max).then_inc(seen_set, 1)
                reached(dve, seen_set, a, 1, 1)
                nc.vector.tensor_scalar(bias_a[a.p][:], seen[:], BIG, -BIG, ALU.mult, ALU.add
                                        ).then_inc(bias_a_set, 1)

            def take_q(a):
                reached(dve, q_mm, a, 1, 1)
                reached(dve, q_lo, a, 1, 1, back=1)
                for m in range(HALVES):
                    nc.vector.scalar_tensor_tensor(out=qf[:, m], in0=ps_a[:, m * TOKENS:(m + 1) * TOKENS],
                                                   scalar=col(a.stage, "q")[:, m:m + 1], in1=some[:],
                                                   op0=ALU.add, op1=ALU.mult).then_inc(q_out, 1)

            def take_v(a):
                reached(dve, v_mm, a, 1, 1)
                reached(dve, handed, a, 2, 2, back=2)
                nc.vector.tensor_tensor(v_a[a.p][:], ps_a[:].rearrange("p (m e) -> p m e", m=HALVES),
                                        bv[:, a.stage:a.stage + 1, :].broadcast_to([P, HALVES, WIDTH]),
                                        ALU.add).then_inc(v_out, 1)

            def row_max(b, slot):
                reached(dve, s_mm, b, HEADS, slot + 1)
                if slot == 0:
                    reached(dve, bias_set, b, 2, 2)
                    reached(dve, m_turned, b, 1, 1, back=2)
                h = head_of(slot)
                apart(dve, dve_passed)
                for q in range(HALVES):
                    at = ps_s[slot % 2][:, q * TOKENS:(q + 1) * TOKENS]
                    nc.vector.tensor_tensor_reduce(at, at, bias[b.p][:, q], 1.0, -HUGE, ALU.add, ALU.max,
                                                   mx[b.p][:, q, h:h + 1]).then_inc(max_set, 1)

            def max_lo(c):
                reached(dve, m_hi, c, 1, 1)
                nc.vector.tensor_tensor(m_parts[:, 1], ps_a[0:HEADS, 0:TOKENS], m_parts[:, 0].bitcast(F32),
                                        ALU.subtract).then_inc(m_lo, 1)

            def normalise(d):
                reached(dve, sums_turned, d, 1, 1)
                reached(dve, normed, d, 2, 2, back=1)
                for q in range(HALVES):
                    of = ps_d[q][:].rearrange("p (s c) -> p s c", c=32)
                    nc.vector.reciprocal(rcp[:, q], of[:, :, HEAD]).then_inc(rcp_set, 1)
                reached(dve, ctx_turned, d, 1, 1, back=1)
                for q in range(HALVES):
                    reached(dve, rcp_set, d, 2, q + 1)
                    of = ps_d[q][:].rearrange("p (j t c) -> p j t c", t=2, c=32)
                    to = ctx_tok[:, q].rearrange("p (t j r) -> p j t r", t=2, r=HEAD)
                    by = rcp[:, q].rearrange("p (j t) -> p j t", t=2)
                    nc.vector.tensor_tensor(to, of[:, :, :, 0:HEAD],
                                            by[:, :, :, None].broadcast_to([P, PAIRS, 2, HEAD]),
                                            ALU.mult).then_inc(normed, 1)

            def residual(d):
                reached(dve, o_mm, d, 1, 1)
                landed(dve, res_ready, d, 16)
                for m in range(HALVES):
                    out = nc.vector.scalar_tensor_tensor(out=res[d.p][:, m], in0=ps_d[1][:, m * TOKENS:(m + 1) * TOKENS],
                                                         scalar=col(d.stage, "o")[:, m:m + 1], in1=res[d.p][:, m],
                                                         op0=ALU.add, op1=ALU.add)
                    if d.stage == 1:
                        out.then_inc(y_set, 1)
                    elif m == HALVES - 1:
                        out.then_inc(d_done, 1)
                    else:
                        out.then_inc(y_set2, 1)

            def ffn_residual(d):
                dve.wait_ge(ffn_mm, d.batch + 1)
                dve.wait_ge(y_set, (d.batch + 1) * 2)
                for m in range(HALVES):
                    out = nc.vector.scalar_tensor_tensor(out=res[d.p][:, m], in0=ps_d[0][:, m * TOKENS:(m + 1) * TOKENS],
                                                         scalar=b2[:, m:m + 1], in1=res[d.p][:, m],
                                                         op0=ALU.add, op1=ALU.add)
                    out.then_inc(d_done if m == HALVES - 1 else z_set, 1)

            def norm(d):
                reached(dve, o_mm, d, 1, 1)
                for m in range(HALVES):
                    nc.vector.bn_stats(stats[:, m], ps_d[1][:, m * WIDTH:(m + 1) * WIDTH]).then_inc(ln_stats, 1)
                for m in range(HALVES):
                    dve.wait_ge(ln_stats, d.batch * 2 + (m + 1))
                    apart(dve, dve_passed)
                    nc.vector.bn_aggr(aggr[:, m], stats[:, m]).then_inc(ln_aggr, 1)
                dve.wait_ge(ln_aggr, (d.batch + 1) * 2)
                nc.vector.tensor_scalar(var_eps[:], aggr[:, :, 1], EPS, None, ALU.add).then_inc(guess, 1)
                dve.wait_ge(guess, d.batch * 3 + 1)
                nc.vector.tensor_scalar(guess_bits[:], var_eps[:].bitcast(I32), 1, None,
                                        ALU.logical_shift_right).then_inc(guess, 1)
                dve.wait_ge(guess, d.batch * 3 + 2)
                nc.vector.tensor_scalar(rstd[:, 0].bitcast(I32), guess_bits[:], -1.0, float(0x5F3759DF),
                                        ALU.mult, ALU.add).then_inc(guess, 1)

            def norm_out(d):
                dve.wait_ge(rstd_set, (d.batch + 1) * NEWTON_OPS)
                landed(dve, res_ready, d, 16)
                for m in range(HALVES):
                    out = nc.vector.tensor_scalar(res[d.p][:, m], ps_d[1][:, m * WIDTH:(m + 1) * WIDTH],
                                                  aggr[:, m, 0:1], rstd[:, NEWTON % 2, m:m + 1], ALU.subtract, ALU.mult)
                    out.then_inc(d_done if m == HALVES - 1 else z_set, 1)
                reached(dve, d_done, d, 1, 1)
                dve.wait_ge(z_set, BATCH + d.batch + 1)
                nc.vector.tensor_tensor(res[d.p][:], res[d.p][:], gamma[:, None, :].broadcast_to([P, HALVES, WIDTH]),
                                        ALU.mult).then_inc(ln_gamma, 1)
                dve.wait_ge(ln_gamma, d.batch + 1)
                nc.vector.tensor_tensor(res[d.p][:], res[d.p][:], beta[:, None, :].broadcast_to([P, HALVES, WIDTH]),
                                        ALU.add).then_inc(ln_out, 1)

            def step(a, b, c, c_before, d):
                for k in range(HEADS):
                    if k == 0 and d.valid:
                        normalise(d)
                    if k == 1 and a.valid:
                        set_allow(a)
                    if k == 1 and c.valid:
                        max_lo(c)
                    if a.valid:
                        if k == 3:
                            set_masks(a)
                        if k == 5:
                            take_q(a)
                        if k == 9:
                            take_v(a)
                    if b.valid:
                        row_max(b, k)
                    if d.valid:
                        if k == 7 and d.stage < 2:
                            residual(d)
                        if k == 7 and d.stage == 2:
                            norm(d)
                        if k == 9 and d.stage == 2:
                            norm_out(d)
                        if k == 15 and d.stage == 1:
                            ffn_residual(d)

            run_steps(dve, step)

        @block.scalar
        def _(act):
            def take_k(a):
                reached(act, k_mm, a, 1, 1)
                reached(act, k_lo, a, 1, 1, back=1)
                for m in range(HALVES):
                    nc.scalar.activation(kf[:, m], ps_a[:, m * TOKENS:(m + 1) * TOKENS], ACT.Identity,
                                         bias=col(a.stage, "k")[:, m:m + 1]).then_inc(k_out, 1)

            def written_before(a):
                if a.u_min >= 1:
                    before = Unit(a.n - (1 - a.p), (a.u_min - 1) // 2, 1 - a.p)
                    landed(act, img_written, before, 16 * 12)

            def part_q(a):
                reached(act, q_out, a, 2, 2)
                written_before(a)
                nc.scalar.copy(q_parts[:, 0], qf[:]).then_inc(q_hi, 1)

            def part_k(a):
                reached(act, k_out, a, 2, 2)
                nc.scalar.copy(k_parts[:, 0], kf[:]).then_inc(k_hi, 1)

            def max_hi(c):
                reached(act, m_turned, c, 1, 1)
                if c.u_min >= 1:
                    before = Unit(c.n - (1 - c.p), (c.u_min - 1) // 2, 1 - c.p)
                    landed(act, m_written, before, 32)
                nc.scalar.copy(m_parts[:, 0], ps_a[0:HEADS, 0:TOKENS]).then_inc(m_hi, 1)

            def hand_over(c):
                reached(act, pv_mm, c, GROUPS, GROUPS, back=2)
                reached(act, v_out, c, 1, 1)
                reached(act, bias_a_set, c, 1, 1)
                for t_ in range(2):
                    src = v_a[c.p][:, :, t_ * P:(t_ + 1) * P].rearrange("p m (j r) -> p m j r", r=HEAD)
                    dst = v_c[c.p][:].rearrange("p m (j t) c -> p t m j c", t=2)[:, t_, :, :, 0:HEAD]
                    out = nc.scalar.copy(dst, src)
                    if t_ == 0:
                        out.then_inc(handed_v, 1)
                    else:
                        out.then_inc(handed, 1)
                reached(act, t_mm, c, HEADS, HEADS, back=2)
                nc.scalar.copy(bias_c[c.p][:], bias_a[c.p][:].rearrange("p t q -> p (t q)")).then_inc(handed, 1)

            def exp(c, slot):
                reached(act, t_mm, c, HEADS, slot + 1)
                if slot % 4 == 0:
                    reached(act, pv_mm, c, GROUPS, slot // 4 + 1, back=1)
                nc.scalar.activation(probs[:, slot // 4, slot % 4], ps_t[slot % 2][:], ACT.Exp,
                                     scale=SCALE).then_inc(exp_done, 1)

            def take_sums(c, half):
                reached(act, pv_mm, c, GROUPS, 2 * half + 2)
                if half == 0:
                    reached(act, sums_turned, c, 1, 1, back=2)
                nc.scalar.copy(sums[c.p][:, 2 * half:2 * half + 2],
                               ps_o[:].rearrange("p (g q) -> p g q", g=2)).then_inc(sums_out, 1)

            def take_ctx(d):
                reached(act, ctx_turned, d, 1, 1)
                reached(act, o_mm, d, 1, 1, back=1)
                nc.scalar.copy(ctx_feat[:], ps_d[0][:].rearrange("p (t q) -> p t q", t=HALVES)).then_inc(ctx_out, 1)

            def relu(d, m2):
                act.wait_ge(hid_mm, d.batch * 4 + (m2 + 1))
                for m in range(2):
                    nc.scalar.activation(hid[:, 2 * m2 + m], ps_d[m2 % 2][:, m * TOKENS:(m + 1) * TOKENS], ACT.Relu,
                                         bias=b1[:, 2 * m2 + m:2 * m2 + m + 1]).then_inc(relu_done, 1)

            def step(a, b, c, c_before, d):
                for k in range(HEADS):
                    if k == 1 and c.valid:
                        max_hi(c)
                    if k == 3 and c.valid:
                        hand_over(c)
                    if a.valid:
                        if k == 6:
                            part_q(a)
                        if k == 7:
                            take_k(a)
                        if k == 8:
                            part_k(a)
                    if k < SHIFT:
                        if c_before.valid:
                            exp(c_before, k + HEADS - SHIFT)
                    elif c.valid:
                        exp(c, k - SHIFT)
                    if c_before.valid and k in (2, 10):
                        take_sums(c_before, k // 8)
                    if d.valid:
                        if k == 4:
                            take_ctx(d)
                        if d.stage == 1 and k in (9, 10, 12, 13):
                            relu(d, (9, 10, 12, 13).index(k))

            act.wait_ge(const_in, 16 * CONSTS)
            act.wait_ge(const_set, 5)
            run_steps(act, step)

        @block.gpsimd
        def _(pool):
            def lo_q(a):
                reached(pool, q_hi, a, 1, 1)
                nc.gpsimd.tensor_tensor(q_parts[:, 1], qf[:], q_parts[:, 0].bitcast(F32), ALU.subtract
                                        ).then_inc(q_lo, 1)

            def lo_k(a):
                reached(pool, k_hi, a, 1, 1)
                nc.gpsimd.tensor_tensor(k_parts[:, 1], kf[:], k_parts[:, 0].bitcast(F32), ALU.subtract
                                        ).then_inc(k_lo, 1)

            def rstd_of(d):
                pool.wait_ge(guess, (d.batch + 1) * 3)
                for i in range(NEWTON):
                    now, new = rstd[:, i % 2], rstd[:, (i + 1) % 2]
                    done = d.batch * NEWTON_OPS + 4 * i
                    nc.gpsimd.tensor_tensor(newton[:, 0], now, now, ALU.mult).then_inc(rstd_set, 1)
                    pool.wait_ge(rstd_set, done + 1)
                    nc.gpsimd.tensor_tensor(newton[:, 1], newton[:, 0], var_eps[:], ALU.mult).then_inc(rstd_set, 1)
                    pool.wait_ge(rstd_set, done + 2)
                    apart(pool, pool_passed)
                    nc.gpsimd.tensor_scalar(newton[:, 2], newton[:, 1], -0.5, 1.5, ALU.mult, ALU.add
                                            ).then_inc(rstd_set, 1)
                    pool.wait_ge(rstd_set, done + 3)
                    nc.gpsimd.tensor_tensor(new, newton[:, 2], now, ALU.mult).then_inc(rstd_set, 1)
                    pool.wait_ge(rstd_set, done + 4)

            def step(a, b, c, c_before, d):
                for k in range(HEADS):
                    if a.valid and k == 7:
                        lo_q(a)
                    if d.valid and d.stage == 2 and k == 8:
                        rstd_of(d)
                    if a.valid and k == 10:
                        lo_k(a)

            run_steps(pool, step)


_OUT = ("out", (BATCH, TOKENS, WIDTH))


def kernel(**inputs):
    from concourse import bacc
    from concourse.bass_utils import run_bass_kernel_spmd

    a = {k: np.asarray(v) for k, v in inputs.items()}

    def columns(v):
        return v.reshape(-1, P).T

    def both(mask):
        return np.stack([np.swapaxes(mask, 1, 2), mask], axis=1)

    def words(mask):
        return np.ascontiguousarray(mask).view(np.int32)

    ins = {
        "x": np.swapaxes(a["x"], 1, 2),
        "ctx": np.swapaxes(a["ctx_1024"], 1, 2),
        "mask0": words(both(a["mask_Bx1xSxS2_bk0"][:, 0])),
        "mask1": words(both(a["mask_Bx1xSxS2_bf1"][:, 0])),
        "mask2": both(a["mask_BxSxS2_ik1"]),
        "w1": a["L0_xattn_W1"], "w2": a["L0_xattn_W2"],
        "b1": columns(a["L0_xattn_b1"]), "b2": columns(a["L0_xattn_b2"]),
        "bv0": a["L0_xattn_sbv"][None], "bv1": a["L0_xattn_cbv"][None],
        "gamma": a["L1_xattn_gamma"][None], "beta": a["L1_xattn_beta"][None],
        "cols": np.concatenate([columns(a[f"L0_xattn_{s}b{c}"]) for s in "sc" for c in "qko"], axis=1),
        "ident": np.eye(P, dtype=np.float32),
    }
    sign = np.zeros((P - STACK_ROWS, HEADS), np.float32)
    sign[0:2, 0:PAIRS] = -1.0
    sign[2:4, PAIRS:HEADS] = -1.0
    ins["max_sign"] = sign
    for c in "qkvo":
        ins[f"w{c}0"] = a[f"L0_xattn_sW{c}"]
        ins[f"w{c}1"] = a[f"L0_xattn_cW{c}"]
        ins[f"w{c}2"] = a[f"L1_xattn_W_{c.upper()}"].T

    nc = bacc.Bacc("TRN2", target_bir_lowering=False, num_devices=1)
    arrays, tensors = {}, {}
    for name, v in ins.items():
        v = np.ascontiguousarray(v)
        arrays[f"in_{name}"] = v
        tensors[name] = nc.dram_tensor(f"in_{name}", v.shape, mybir.dt.from_np(v.dtype), kind="ExternalInput").ap()
    tensors["out"] = nc.dram_tensor("out", _OUT[1], F32, kind="ExternalOutput").ap()
    build(nc, tensors)
    return run_bass_kernel_spmd(nc, [arrays], core_ids=[0]).results[0]["out"]
```

```python
from contextlib import ExitStack

import numpy as np

import concourse.bass as bass
from concourse import mybir

P = 128
BATCH, TOKENS, WIDTH, HEADS, HIDDEN = 8, 256, 256, 16, 1024
HEAD = WIDTH // HEADS
STAGES = 3
UNITS = STAGES * BATCH
HALVES = WIDTH // P
PAIRS = HEADS // 2
PARTS = 3
HALF_ROWS = PARTS * HEAD
STACK_ROWS = 2 * HALF_ROWS
MAX_ROWS = STACK_ROWS + 4
GROUPS = 4
SHIFT = 6
WEIGH_AFTER = 5
AT = {
    "pe_turn_sums": 0, "dve_normalise": (0, 1), "pe_turn_ctx": 2, "act_take_ctx": 4, "pe_project_out": 6,
    "dve_residual": 7, "dve_norm": 6, "pool_rstd": 12, "dve_norm_out": (11, 12, 13), "pe_hidden": (9, 12, 12, 13),
    "act_relu": (9, 10, 12, 13), "pe_ffn_out": (13, 14, 14, 14), "dve_ffn_residual": (12, 13), "pe_turn_max": 0,
    "act_max_hi": 1, "dve_max_lo": 2, "act_hand_over": 4, "dve_allow": 3, "pe_count": 4, "dve_masks": (4, 4, 4),
    "pe_q": 4, "dve_take_q": 4, "act_part_q": 4, "pool_lo_q": 8, "pe_k": 6, "act_take_k": 7, "act_part_k": 7,
    "pool_lo_k": 10, "pe_v": 8, "dve_take_v": 9,
}
SCALE = HEAD ** -0.5
BIG = 1.0e30
HUGE = 3.0e38
EPS = 1e-5
NEWTON = 3
NEWTON_OPS = 4 * NEWTON

F32 = mybir.dt.float32
F32R = mybir.dt.float32r
BF16 = mybir.dt.bfloat16
U8 = mybir.dt.uint8
I32 = mybir.dt.int32
ALU = mybir.AluOpType
ACT = mybir.ActivationFunctionType


class Unit:

    def __init__(self, n, n_min, p):
        self.n, self.p = n, p
        self.u = n * 2 + p
        self.u_min = 2 * n_min + p
        self.stage = self.u_min // BATCH
        self.valid = 0 <= self.u_min < UNITS
        self.batch = self.u - BATCH * self.stage


def reached(eng, sem, unit, per, count, back=0):
    least = per * (unit.u_min - back) + count
    if unit.u_min - back >= 0 and least > 0:
        eng.wait_ge(sem, unit.u * per + (count - per * back))


def landed(eng, sem, unit, per, back=0):
    if unit.u_min - 2 * back >= 0:
        eng.wait_ge(sem[unit.p], (unit.n - back + 1) * per)


def apart(eng, sem):
    eng.sem_inc(sem, 1)


def steps():
    def work(i):
        out = []
        for par in range(2):
            for ahead in (2, 1, 0, -1, -2):
                u = 2 * i + par + ahead
                has_stage = ahead in (2, -2) and 0 <= u < UNITS
                out.append((u // BATCH if has_stage else 0 <= u < UNITS, u >= 2))
        return out

    runs = []
    for i in range(-1, UNITS // 2 + 1):
        if runs and work(i) == work(runs[-1][0]):
            runs[-1][1] = i + 1
        else:
            runs.append([i, i + 1])
    return runs


def run_steps(eng, body, before=None):
    for run, (first, end) in enumerate(steps()):
        if before and run in before:
            before[run]()
        def two_steps(i):
            for par in range(2):
                def at(ahead):
                    o = par + ahead
                    return Unit(i + o // 2, first + o // 2, o % 2)
                body(at(2), at(1), at(0), at(-1), at(-2))
        if end - first == 1:
            two_steps(first)
        else:
            with eng.Fori(first, end) as i:
                two_steps(i)


def head_of(slot):
    return slot // 2 + (slot % 2) * PAIRS


def build(nc, t):
    ctx = ExitStack()
    with ctx:
        def sb(name, shape, dt=F32):
            return ctx.enter_context(nc.sbuf_tensor(name, shape, dt))

        def sem(name):
            return ctx.enter_context(nc.semaphore(name))

        def sem2(name):
            return [sem(f"{name}{p}") for p in range(2)]

        def two(name, shape, dt=F32):
            return [sb(f"{name}{p}", shape, dt) for p in range(2)]

        w = [{c: sb(f"w{c}{s}", [P, HALVES, WIDTH]) for c in "qkvo"} for s in range(STAGES)]
        w1 = sb("w1", [P, HALVES, HIDDEN])
        w2 = sb("w2", [P, HIDDEN // P, WIDTH])
        cols = sb("cols", [P, 2 * 3 * HALVES])
        zero_col = sb("zero_col", [P, HALVES])
        b1 = sb("b1", [P, HIDDEN // P])
        b2 = sb("b2", [P, HALVES])
        bv = sb("bv", [P, STAGES, WIDTH])
        gamma = sb("gamma", [P, WIDTH])
        beta = sb("beta", [P, WIDTH])
        ident = sb("ident", [P, P])
        ones = sb("ones", [P, P], BF16)
        max_sign = sb("max_sign", [P, HEADS])
        xq = two("xq", [P, HALVES, TOKENS])
        xkv = two("xkv", [P, HALVES, TOKENS])
        raw32 = two("raw32", [P, 2, HALVES, TOKENS], I32)
        raw_words = [r[:, :, :, 0:TOKENS // 4] for r in raw32]
        raw8 = [r[:].bitcast(U8)[:, :, :, 0:TOKENS] for r in raw32]
        allow = sb("allow", [P, 2, HALVES, TOKENS], BF16)
        some = sb("some", [P, TOKENS], BF16)
        none = sb("none", [P, TOKENS], BF16)
        some_big = sb("some_big", [P, HALVES])
        bias = two("bias", [P, HALVES, TOKENS], BF16)
        seen = sb("seen", [P, HALVES, TOKENS], BF16)
        ident16 = sb("ident16", [P, P], BF16)
        bias_a = two("bias_a", [P, HALVES, TOKENS], BF16)
        v_a = two("v_a", [P, HALVES, WIDTH])
        qf = sb("qf", [P, HALVES, TOKENS])
        kf = sb("kf", [P, HALVES, TOKENS])
        q_parts = sb("q_parts", [P, 2, HALVES, TOKENS], F32R)
        k_parts = sb("k_parts", [P, 2, HALVES, TOKENS], F32R)
        q_stack = two("q_stack", [P, PAIRS, TOKENS], F32R)
        k_stack = two("k_stack", [P, HEADS, TOKENS], F32R)
        mx = two("mx", [P, HALVES, HEADS])
        m_parts = sb("m_parts", [HEADS, 2, TOKENS], F32R)
        probs = sb("probs", [P, 2, 4, HALVES * TOKENS])
        bias_c = two("bias_c", [P, HALVES * TOKENS], BF16)
        v_c = two("v_c", [P, HALVES, HEADS, 32])
        sums = two("sums", [P, GROUPS, TOKENS])
        rcp = sb("rcp", [P, HALVES, HEADS])
        ctx_tok = sb("ctx_tok", [P, HALVES, WIDTH])
        ctx_feat = sb("ctx_feat", [P, HALVES, TOKENS])
        res = two("res", [P, HALVES, TOKENS])
        hid = sb("hid", [P, HIDDEN // P, TOKENS])
        stats = sb("stats", [P, HALVES, 6])
        aggr = sb("aggr", [P, HALVES, 2])
        var_eps = sb("var_eps", [P, HALVES])
        guess_bits = sb("guess_bits", [P, HALVES], I32)
        rstd = sb("rstd", [P, 2, HALVES])
        newton = sb("newton", [P, 3, HALVES])

        def bank(name):
            return ctx.enter_context(nc.psum_tensor(name, [P, 512], F32))

        ps_a = bank("ps_a")
        ps_s = [bank(f"ps_s{i}") for i in range(2)]
        ps_t = [bank(f"ps_t{i}") for i in range(2)]
        ps_o = bank("ps_o")
        ps_d = [bank(f"ps_d{i}") for i in range(2)]

        x_wait = nc.dram_tensor("x_wait", [UNITS, WIDTH, TOKENS], F32).ap()
        q_img = nc.dram_tensor("q_img", [2, 2, PARTS, HEAD, PAIRS, TOKENS], F32).ap()
        k_img = nc.dram_tensor("k_img", [2, 2, PARTS, HEAD, PAIRS, TOKENS], F32).ap()
        m_img = nc.dram_tensor("m_img", [2, 2, 2, PAIRS, TOKENS], F32).ap()

        first_in, signs_in, wo_in, late_in = sem("first_in"), sem("signs_in"), sem("wo_in"), sem("late_in")
        const_set, signs_set, k_zeroed = sem("const_set"), sem("signs_set"), sem2("k_zeroed")
        in_ready = sem2("in_ready")
        img_written = sem2("img_written")
        stack_ready = [sem2("stack_ready_lo"), sem2("stack_ready_hi")]
        m_written, m_ready = sem2("m_written"), sem2("m_ready")
        res_ready, stored = sem2("res_ready"), sem2("stored")
        count_mm, q_mm, k_mm, v_mm = sem("count_mm"), sem("q_mm"), sem("k_mm"), sem("v_mm")
        m_turned, s_mm, t_mm, pv_mm = sem("m_turned"), sem("s_mm"), sem("t_mm"), sem("pv_mm")
        sums_turned, ctx_turned, o_mm = sem("sums_turned"), sem("ctx_turned"), sem("o_mm")
        hid_mm, ffn_mm = sem("hid_mm"), sem("ffn_mm")
        allow_set, some_set, none_set, big_set = sem("allow_set"), sem("some_set"), sem("none_set"), sem("big_set")
        bias_a_set, bias_set, q_out, v_out = sem("bias_a_set"), sem("bias_set"), sem("q_out"), sem("v_out")
        max_set, m_lo, rcp_set, normed = sem("max_set"), sem("m_lo"), sem("rcp_set"), sem("normed")
        y_set, y_set2, z_set, handed_v = sem("y_set"), sem("y_set2"), sem("z_set"), sem("handed_v")
        d_done, ln_stats, ln_aggr, ln_gamma, ln_out = (
            sem("d_done"), sem("ln_stats"), sem("ln_aggr"), sem("ln_gamma"), sem("ln_out"))
        k_out, q_hi, k_hi, m_hi, exp_done = sem("k_out"), sem("q_hi"), sem("k_hi"), sem("m_hi"), sem("exp_done")
        sums_out, ctx_out, handed, relu_done = sem("sums_out"), sem("ctx_out"), sem("handed"), sem("relu_done")
        q_lo, k_lo, rstd_set = sem("q_lo"), sem("k_lo"), sem("rstd_set")
        dve_passed, pool_passed, sp_passed = sem("dve_passed"), sem("pool_passed"), sem("sp_passed")
        guess, seen_set = sem("guess"), sem("seen_set")

        FIRST, LATE = 5, 4 * (STAGES - 1) + 2 + 2 + 1 + 2

        def col(stage, which):
            if stage == 2:
                return zero_col
            o = (3 * stage + "qko".index(which)) * HALVES
            return cols[:, o:o + HALVES]

        def feat(ap):
            return ap.rearrange("(t p) q -> p t q", p=P)

        block = ctx.enter_context(nc.Block())

        @block.sync
        def _(sp):
            sp.dma_start(w[0]["q"][:], feat(t["wq0"])).then_inc(first_in, 16)
            sp.dma_start(cols[:], t["cols"]).then_inc(first_in, 16)

            def load(a):
                reached(sp, v_mm, a, 1, 1, back=2)
                apart(sp, sp_passed)
                reached(sp, allow_set, a, 2, 2, back=2)
                apart(sp, sp_passed)
                x_in = t["x"][a.batch] if a.stage == 0 else x_wait[a.u]
                if a.stage > 0:
                    landed(sp, stored, a, 16, back=BATCH // 2)
                    apart(sp, sp_passed)
                sp.dma_start(xq[a.p][:], feat(x_in)).then_inc(in_ready[a.p], 16)
                kv_in = t["x"][a.batch] if a.stage == 0 else t["ctx"][a.batch]
                sp.dma_start(xkv[a.p][:], feat(kv_in)).then_inc(in_ready[a.p], 16)
                raw = raw32 if a.stage == 2 else raw_words
                for o in range(2):
                    sp.dma_start(raw[a.p][:, o], t[f"mask{a.stage}"][a.batch, o].rearrange("(t p) q -> p t q", p=P)
                                 ).then_inc(in_ready[a.p], 16)

            def write_stacks(a):
                landed(sp, stack_ready[0], a, 48, back=1)
                apart(sp, sp_passed)
                landed(sp, stack_ready[1], a, 48, back=1)
                apart(sp, sp_passed)
                for parts, img, order, done in ((q_parts, q_img, (0, 0, 1), q_lo), (k_parts, k_img, (0, 1, 0), k_lo)):
                    reached(sp, done, a, 1, 1)
                    apart(sp, sp_passed)
                    for c, part in enumerate(order):
                        dst = img[a.p, :, c].rearrange("t r j q -> j r t q")
                        for t_ in range(HALVES):
                            sp.dma_start(dst[:, :, t_, :], parts[:, part, t_, :].bitcast(F32)).then_inc(img_written[a.p], 16)

            def read_stacks(a, g):
                landed(sp, img_written, a, 16 * 12)
                apart(sp, sp_passed)
                if a.u_min < 2 and g == 0:
                    sp.wait_ge(k_zeroed[a.p], 1)
                reached(sp, t_mm, a, HEADS, 8 * g + 8, back=2)
                apart(sp, sp_passed)
                j = slice(4 * g, 4 * g + 4)
                sem_ = stack_ready[g][a.p]
                sp.dma_start(q_stack[a.p][0:STACK_ROWS, j, :].bitcast(F32),
                             q_img[a.p].rearrange("t c r j q -> (t c r) j q")[:, j, :]).then_inc(sem_, 16)
                for half in range(2):
                    sp.dma_start(k_stack[a.p][half * HALF_ROWS:(half + 1) * HALF_ROWS,
                                              half * PAIRS + 4 * g:half * PAIRS + 4 * g + 4, :].bitcast(F32),
                                 k_img[a.p, half].rearrange("c r j q -> (c r) j q")[:, j, :]).then_inc(sem_, 16)

            def pass_max(c):
                landed(sp, m_ready, c, 16, back=1)
                apart(sp, sp_passed)
                reached(sp, m_lo, c, 1, 1)
                apart(sp, sp_passed)
                for half in range(2):
                    sp.dma_start(m_img[c.p, half].rearrange("c j q -> j c q"),
                                 m_parts[half * PAIRS:(half + 1) * PAIRS].bitcast(F32)).then_inc(m_written[c.p], 16)
                landed(sp, m_written, c, 32)
                apart(sp, sp_passed)
                reached(sp, t_mm, c, HEADS, HEADS, back=2)
                apart(sp, sp_passed)
                sp.dma_start(q_stack[c.p][STACK_ROWS:MAX_ROWS].bitcast(F32),
                             m_img[c.p].rearrange("t c j q -> (t c) j q")).then_inc(m_ready[c.p], 16)

            def load_res(d):
                landed(sp, stored, d, 16, back=1)
                apart(sp, sp_passed)
                x_in = t["x"][d.batch] if d.stage == 0 else x_wait[d.u]
                sp.dma_start(res[d.p][:], feat(x_in)).then_inc(res_ready[d.p], 16)

            def store(d):
                if d.stage == 2:
                    eng_out = t["out"][d.batch].rearrange("(t p) e -> p t e", p=P)
                    sp.wait_ge(ln_out, d.batch + 1)
                    apart(sp, sp_passed)
                    sp.dma_start(eng_out, res[d.p][:]).then_inc(stored[d.p], 16)
                else:
                    reached(sp, d_done, d, 1, 1)
                    apart(sp, sp_passed)
                    sp.dma_start(feat(x_wait[d.u + BATCH]), res[d.p][:]
                                 ).then_inc(stored[d.p], 16)

            def step(a, b, c, c_before, d):
                if a.valid and a.u_min >= 2:
                    load(a)
                if d.valid:
                    load_res(d)
                if c.valid:
                    pass_max(c)
                if b.valid:
                    read_stacks(b, 1)
                if a.valid:
                    write_stacks(a)
                if a.valid:
                    read_stacks(a, 0)
                if d.valid:
                    store(d)

            def load_first():
                load(Unit(0, 0, 0))
                load(Unit(0, 0, 1))

            run_steps(sp, step, {0: load_first})
            for p in range(2):
                sp.wait_ge(stored[p], 16 * UNITS // 2)

        @block.tensor
        def _(pe):
            mm = nc.tensor.matmul

            def count_keys(a):
                reached(pe, allow_set, a, 2, 1)
                reached(pe, v_out, a, 1, 1, back=1)
                reached(pe, m_lo, a, 1, 1, back=2)
                for k in range(HALVES):
                    mm(ps_a[:, 0:TOKENS], ones[:], allow[:, 0, k, :], start=(k == 0), stop=(k == HALVES - 1))
                for q in range(HALVES):
                    for k in range(HALVES):
                        last = mm(ps_a[:, TOKENS + 2 * q:TOKENS + 2 * q + 2], allow[:, 0, k, q * P:(q + 1) * P],
                                  ones[:, 0:2], start=(k == 0), stop=(k == HALVES - 1))
                last.then_inc(count_mm, 1)

            def project(weights, moving, done):
                for m in range(HALVES):
                    for k in range(HALVES):
                        last = mm(ps_a[:, m * TOKENS:(m + 1) * TOKENS], weights[:, k, m * P:(m + 1) * P],
                                  moving[:, k, :], start=(k == 0), stop=(k == HALVES - 1))
                last.then_inc(done, 1)

            def project_q(a):
                landed(pe, in_ready, a, 64)
                reached(pe, some_set, a, 1, 1)
                reached(pe, big_set, a, 1, 1)
                project(w[a.stage]["q"], xq[a.p], q_mm)

            def project_k(a):
                reached(pe, q_out, a, 2, 2)
                project(w[a.stage]["k"], xkv[a.p], k_mm)

            def project_v(a):
                reached(pe, k_out, a, 2, 2)
                for m in range(HALVES):
                    for k in range(HALVES):
                        last = mm(ps_a[:, m * WIDTH:(m + 1) * WIDTH], xkv[a.p][:, k, m * P:(m + 1) * P],
                                  w[a.stage]["v"][:, k, :], start=(k == 0), stop=(k == HALVES - 1))
                last.then_inc(v_mm, 1)

            def scores(b, slot):
                if slot % 8 == 0:
                    landed(pe, stack_ready[slot // 8], b, 48)
                reached(pe, max_set, b, 2 * HEADS, 2 * slot - 2)
                if slot < 2:
                    reached(pe, max_set, b, 2 * HEADS, 2 * HEADS + 2 * slot - 2, back=1)
                for q in range(HALVES):
                    last = mm(ps_s[slot % 2][:, q * TOKENS:(q + 1) * TOKENS],
                              q_stack[b.p][0:STACK_ROWS, slot // 2, q * P:(q + 1) * P],
                              k_stack[b.p][0:STACK_ROWS, head_of(slot), :], start=True, stop=True)
                last.then_inc(s_mm, 1)

            def turn_max(c):
                reached(pe, max_set, c, 2 * HEADS, 2 * HEADS)
                reached(pe, v_out, c, 1, 1)
                if c.u_min + 1 < UNITS:
                    reached(pe, v_out, c, 1, 2)
                for q in range(HALVES):
                    last = nc.tensor.transpose(ps_a[0:HEADS, q * P:(q + 1) * P], mx[c.p][:, q, :], ident[:])
                last.then_inc(m_turned, 1)

            def scores_less_max(c, slot):
                if slot == 0:
                    landed(pe, m_ready, c, 16)
                    reached(pe, handed, c, 2, 2)
                reached(pe, exp_done, c, HEADS, slot - 1)
                if slot < 1:
                    reached(pe, exp_done, c, HEADS, HEADS + slot - 1, back=1)
                mm(ps_t[slot % 2][:], ident16[:], bias_c[c.p][:], start=True, stop=False, skip_group_check=True)
                for k in range(HALVES):
                    last = mm(ps_t[slot % 2][:, k * TOKENS:(k + 1) * TOKENS],
                              k_stack[c.p][0:MAX_ROWS, head_of(slot), k * P:(k + 1) * P],
                              q_stack[c.p][0:MAX_ROWS, slot // 2, :], start=False, stop=(k == HALVES - 1),
                              skip_group_check=True)
                last.then_inc(t_mm, 1)

            def weigh_values(c, g):
                reached(pe, exp_done, c, HEADS, 4 * g + 4)
                if g == 0:
                    reached(pe, handed, c, 2, 2)
                if g % 2 == 0:
                    reached(pe, sums_out, c, 2, g // 2)
                for k in range(HALVES):
                    for j in range(4):
                        last = mm(ps_o[32 * j:32 * j + 32, (g % 2) * TOKENS:(g % 2 + 1) * TOKENS],
                                  v_c[c.p][:, k, 4 * g + j, :], probs[:, g % 2, j, k * TOKENS:(k + 1) * TOKENS],
                                  start=(k == 0), stop=(k == HALVES - 1), tile_position=(0, 32 * j))
                last.then_inc(pv_mm, 1)

            def turn_sums(d):
                reached(pe, sums_out, d, 2, 2)
                reached(pe, d_done, d, 1, 1, back=1)
                for q in range(HALVES):
                    for g in range(GROUPS):
                        last = nc.tensor.transpose(ps_d[q][:, g * P:(g + 1) * P],
                                                   sums[d.p][:, g, q * P:(q + 1) * P], ident[:])
                last.then_inc(sums_turned, 1)

            def turn_ctx(d):
                reached(pe, normed, d, 2, 2)
                for f in range(HALVES):
                    for q in range(HALVES):
                        last = nc.tensor.transpose(ps_d[0][:, f * TOKENS + q * P:f * TOKENS + (q + 1) * P],
                                                   ctx_tok[:, q, f * P:(f + 1) * P], ident[:])
                last.then_inc(ctx_turned, 1)

            def project_out(d):
                reached(pe, ctx_out, d, 1, 1)
                wo = w[d.stage]["o"]
                if d.stage < 2:
                    for m in range(HALVES):
                        for k in range(HALVES):
                            last = mm(ps_d[1][:, m * TOKENS:(m + 1) * TOKENS], wo[:, k, m * P:(m + 1) * P],
                                      ctx_feat[:, k, :], start=(k == 0), stop=(k == HALVES - 1))
                else:
                    landed(pe, res_ready, d, 16)
                    for m in range(HALVES):
                        for k in range(HALVES):
                            mm(ps_d[1][:, m * WIDTH:(m + 1) * WIDTH], ctx_feat[:, k, m * P:(m + 1) * P],
                               wo[:, k, :], start=(k == 0), stop=False, skip_group_check=True)
                        for k in range(HALVES):
                            last = mm(ps_d[1][:, m * WIDTH + k * P:m * WIDTH + (k + 1) * P],
                                      res[d.p][:, k, m * P:(m + 1) * P], ident[:], start=False,
                                      stop=(k == HALVES - 1), skip_group_check=True)
                last.then_inc(o_mm, 1)

            def hidden(d, m2):
                if m2 == 0:
                    pe.wait_ge(y_set, (d.batch + 1) * 2)
                elif m2 > 1:
                    pe.wait_ge(relu_done, d.batch * 8 + 2 * (m2 - 1))
                for m in range(2):
                    for k in range(HALVES):
                        o = (2 * m2 + m) * P
                        last = mm(ps_d[m2 % 2][:, m * TOKENS:(m + 1) * TOKENS], w1[:, k, o:o + P],
                                  res[d.p][:, k, :], start=(k == 0), stop=(k == HALVES - 1))
                last.then_inc(hid_mm, 1)

            def ffn_out(d, piece):
                m, part = divmod(piece, 2)
                if piece == 0:
                    pe.wait_ge(relu_done, (d.batch + 1) * 8)
                for k in range(4 * part, 4 * part + 4):
                    last = mm(ps_d[m][:, 0:TOKENS], w2[:, k, m * P:(m + 1) * P],
                              hid[:, k, :], start=(k == 0), stop=(k == HIDDEN // P - 1))
                if part == 1:
                    last.then_inc(ffn_mm, 1)

            def step(a, b, c, c_before, d):
                for k in range(HEADS):
                    if d.valid and k == AT["pe_turn_sums"]:
                        turn_sums(d)
                    if c.valid and k == AT["pe_turn_max"]:
                        turn_max(c)
                    if a.valid and k == AT["pe_count"]:
                        count_keys(a)
                    if a.valid and k == AT["pe_q"]:
                        project_q(a)
                    if a.valid and k == AT["pe_k"]:
                        project_k(a)
                    if a.valid and k == AT["pe_v"]:
                        project_v(a)
                    if b.valid:
                        scores(b, k)
                    if k < SHIFT and c_before.valid:
                        scores_less_max(c_before, k + HEADS - SHIFT)
                    if k >= SHIFT and c.valid:
                        scores_less_max(c, k - SHIFT)
                    for g in range(GROUPS):
                        at = SHIFT + 4 * g + WEIGH_AFTER
                        of = c if at < HEADS else c_before
                        if of.valid and k == at % HEADS:
                            weigh_values(of, g)
                    if d.valid and k == AT["pe_turn_ctx"]:
                        turn_ctx(d)
                    if d.valid and k == AT["pe_project_out"]:
                        project_out(d)
                    if d.valid and d.stage == 1:
                        for m2 in range(4):
                            if k == AT["pe_hidden"][m2]:
                                hidden(d, m2)
                        for piece in range(4):
                            if k == AT["pe_ffn_out"][piece]:
                                ffn_out(d, piece)

            def all_set():
                pe.wait_ge(signs_in, 32)
                pe.wait_ge(signs_set, 3)
                pe.wait_ge(wo_in, 16)

            pe.wait_ge(first_in, 16 * FIRST)
            pe.wait_ge(const_set, 5)
            run_steps(pe, step, {1: all_set, 2: lambda: pe.wait_ge(late_in, 16 * LATE)})

        @block.vector
        def _(dve):
            nc.vector.memset(zero_col[:], 0.0).then_inc(const_set, 1)
            nc.vector.memset(ones[:], 1.0).then_inc(const_set, 1)
            nc.vector.memset(bv[:, 2, :], 0.0).then_inc(const_set, 1)
            for p in range(2):
                nc.vector.memset(v_c[p][:, :, :, HEAD:32], 1.0).then_inc(const_set, 1)
            nc.vector.memset(k_stack[0][0:STACK_ROWS].bitcast(F32), 0.0).then_inc(k_zeroed[0], 1)
            dve.wait_ge(signs_in, 32)
            nc.vector.tensor_copy(ident16[:], ident[:]).then_inc(signs_set, 1)
            dve.wait_ge(const_set, 5)
            dve.wait_ge(first_in, 16 * FIRST)

            def set_allow(a):
                landed(dve, in_ready, a, 64)
                reached(dve, count_mm, a, 1, 1, back=1)
                reached(dve, bias_a_set, a, 1, 1, back=1)
                reached(dve, bias_set, a, 2, 2, back=1)
                raw, blocked = (raw32, 1.0) if a.stage == 2 else (raw8, 0.0)
                for o in range(2):
                    nc.vector.tensor_scalar(allow[:, o], raw[a.p][:, o], blocked, None,
                                            ALU.not_equal).then_inc(allow_set, 1)

            def set_some(a):
                reached(dve, count_mm, a, 1, 1)
                reached(dve, q_out, a, 2, 2, back=1)
                reached(dve, bias_a_set, a, 1, 1, back=1)
                nc.vector.tensor_scalar(some[:], ps_a[:, 0:TOKENS], 1.0, None, ALU.min).then_inc(some_set, 1)
                nc.vector.tensor_scalar(
                    some_big[:], ps_a[:, TOKENS:TOKENS + 4].rearrange("p (q two) -> p q two", two=2)[:, :, 0],
                    1.0, BIG, ALU.min, ALU.mult).then_inc(big_set, 1)

            def set_bias(a):
                reached(dve, some_set, a, 1, 1)
                nc.vector.tensor_scalar(none[:], some[:], -1.0, 1.0, ALU.mult, ALU.add).then_inc(none_set, 1)
                reached(dve, big_set, a, 1, 1)
                reached(dve, allow_set, a, 2, 2)
                reached(dve, max_set, a, 2 * HEADS, 2 * HEADS, back=2)
                for q in range(HALVES):
                    nc.vector.tensor_scalar(bias[a.p][:, q], allow[:, 1, q], some_big[:, q:q + 1],
                                            some_big[:, q:q + 1], ALU.mult, ALU.subtract).then_inc(bias_set, 1)

            def set_bias_a(a):
                reached(dve, none_set, a, 1, 1)
                reached(dve, handed, a, 2, 2, back=2)
                nc.vector.tensor_tensor(seen[:], allow[:, 0], none[:, None, :].broadcast_to([P, HALVES, TOKENS]),
                                        ALU.max).then_inc(seen_set, 1)
                reached(dve, seen_set, a, 1, 1)
                nc.vector.tensor_scalar(bias_a[a.p][:], seen[:], BIG, -BIG, ALU.mult, ALU.add
                                        ).then_inc(bias_a_set, 1)

            def take_q(a):
                reached(dve, q_mm, a, 1, 1)
                reached(dve, q_lo, a, 1, 1, back=1)
                for m in range(HALVES):
                    nc.vector.scalar_tensor_tensor(out=qf[:, m], in0=ps_a[:, m * TOKENS:(m + 1) * TOKENS],
                                                   scalar=col(a.stage, "q")[:, m:m + 1], in1=some[:],
                                                   op0=ALU.add, op1=ALU.mult).then_inc(q_out, 1)

            def take_v(a):
                reached(dve, v_mm, a, 1, 1)
                reached(dve, handed, a, 2, 2, back=2)
                nc.vector.tensor_tensor(v_a[a.p][:], ps_a[:].rearrange("p (m e) -> p m e", m=HALVES),
                                        bv[:, a.stage:a.stage + 1, :].broadcast_to([P, HALVES, WIDTH]),
                                        ALU.add).then_inc(v_out, 1)

            def row_max(b, slot):
                reached(dve, s_mm, b, HEADS, slot + 1)
                if slot == 0:
                    reached(dve, bias_set, b, 2, 2)
                    reached(dve, m_turned, b, 1, 1, back=2)
                h = head_of(slot)
                apart(dve, dve_passed)
                for q in range(HALVES):
                    at = ps_s[slot % 2][:, q * TOKENS:(q + 1) * TOKENS]
                    nc.vector.tensor_tensor_reduce(at, at, bias[b.p][:, q], 1.0, -HUGE, ALU.add, ALU.max,
                                                   mx[b.p][:, q, h:h + 1]).then_inc(max_set, 1)

            def max_lo(c):
                reached(dve, m_hi, c, 1, 1)
                nc.vector.tensor_tensor(m_parts[:, 1], ps_a[0:HEADS, 0:TOKENS], m_parts[:, 0].bitcast(F32),
                                        ALU.subtract).then_inc(m_lo, 1)

            def normalise(d, q):
                reached(dve, sums_turned, d, 1, 1)
                reached(dve, normed, d, 2, 2, back=1)
                nc.vector.reciprocal(rcp[:, q], ps_d[q][:].rearrange("p (s c) -> p s c", c=32)[:, :, HEAD]
                                     ).then_inc(rcp_set, 1)
                reached(dve, ctx_turned, d, 1, 1, back=1)
                reached(dve, rcp_set, d, 2, q + 1)
                of = ps_d[q][:].rearrange("p (j t c) -> p j t c", t=2, c=32)
                to = ctx_tok[:, q].rearrange("p (t j r) -> p j t r", t=2, r=HEAD)
                by = rcp[:, q].rearrange("p (j t) -> p j t", t=2)
                nc.vector.tensor_tensor(to, of[:, :, :, 0:HEAD], by[:, :, :, None].broadcast_to([P, PAIRS, 2, HEAD]),
                                        ALU.mult).then_inc(normed, 1)

            def residual(d):
                reached(dve, o_mm, d, 1, 1)
                landed(dve, res_ready, d, 16)
                for m in range(HALVES):
                    out = nc.vector.scalar_tensor_tensor(out=res[d.p][:, m], in0=ps_d[1][:, m * TOKENS:(m + 1) * TOKENS],
                                                         scalar=col(d.stage, "o")[:, m:m + 1], in1=res[d.p][:, m],
                                                         op0=ALU.add, op1=ALU.add)
                    if d.stage == 1:
                        out.then_inc(y_set, 1)
                    elif m == HALVES - 1:
                        out.then_inc(d_done, 1)
                    else:
                        out.then_inc(y_set2, 1)

            def ffn_residual(d, m):
                dve.wait_ge(ffn_mm, d.batch * 2 + (m + 1))
                if m == 0:
                    dve.wait_ge(y_set, (d.batch + 1) * 2)
                out = nc.vector.scalar_tensor_tensor(out=res[d.p][:, m], in0=ps_d[m][:, 0:TOKENS],
                                                     scalar=b2[:, m:m + 1], in1=res[d.p][:, m],
                                                     op0=ALU.add, op1=ALU.add)
                out.then_inc(d_done if m == HALVES - 1 else z_set, 1)

            def norm(d):
                reached(dve, o_mm, d, 1, 1)
                for m in range(HALVES):
                    nc.vector.bn_stats(stats[:, m], ps_d[1][:, m * WIDTH:(m + 1) * WIDTH]).then_inc(ln_stats, 1)
                for m in range(HALVES):
                    dve.wait_ge(ln_stats, d.batch * 2 + (m + 1))
                    apart(dve, dve_passed)
                    nc.vector.bn_aggr(aggr[:, m], stats[:, m]).then_inc(ln_aggr, 1)
                dve.wait_ge(ln_aggr, (d.batch + 1) * 2)
                nc.vector.tensor_scalar(var_eps[:], aggr[:, :, 1], EPS, None, ALU.add).then_inc(guess, 1)
                dve.wait_ge(guess, d.batch * 3 + 1)
                nc.vector.tensor_scalar(guess_bits[:], var_eps[:].bitcast(I32), 1, None,
                                        ALU.logical_shift_right).then_inc(guess, 1)
                dve.wait_ge(guess, d.batch * 3 + 2)
                nc.vector.tensor_scalar(rstd[:, 0].bitcast(I32), guess_bits[:], -1.0, float(0x5F3759DF),
                                        ALU.mult, ALU.add).then_inc(guess, 1)

            def norm_out(d, part):
                dve.wait_ge(rstd_set, (d.batch + 1) * NEWTON_OPS)
                if part == 0:
                    landed(dve, res_ready, d, 16)
                    for m in range(HALVES):
                        out = nc.vector.tensor_scalar(res[d.p][:, m], ps_d[1][:, m * WIDTH:(m + 1) * WIDTH],
                                                      aggr[:, m, 0:1], rstd[:, NEWTON % 2, m:m + 1],
                                                      ALU.subtract, ALU.mult)
                        out.then_inc(d_done if m == HALVES - 1 else z_set, 1)
                elif part == 1:
                    reached(dve, d_done, d, 1, 1)
                    dve.wait_ge(z_set, BATCH + d.batch + 1)
                    nc.vector.tensor_tensor(res[d.p][:], res[d.p][:],
                                            gamma[:, None, :].broadcast_to([P, HALVES, WIDTH]),
                                            ALU.mult).then_inc(ln_gamma, 1)
                else:
                    dve.wait_ge(ln_gamma, d.batch + 1)
                    nc.vector.tensor_tensor(res[d.p][:], res[d.p][:],
                                            beta[:, None, :].broadcast_to([P, HALVES, WIDTH]),
                                            ALU.add).then_inc(ln_out, 1)

            def step(a, b, c, c_before, d):
                for k in range(HEADS):
                    for q in range(HALVES):
                        if d.valid and k == AT["dve_normalise"][q]:
                            normalise(d, q)
                    if a.valid and k == AT["dve_allow"]:
                        set_allow(a)
                    if c.valid and k == AT["dve_max_lo"]:
                        max_lo(c)
                    for part, set_part in enumerate((set_some, set_bias, set_bias_a)):
                        if a.valid and k == AT["dve_masks"][part]:
                            set_part(a)
                    if a.valid and k == AT["dve_take_q"]:
                        take_q(a)
                    if a.valid and k == AT["dve_take_v"]:
                        take_v(a)
                    if b.valid:
                        row_max(b, k)
                    if d.valid and d.stage < 2 and k == AT["dve_residual"]:
                        residual(d)
                    if d.valid and d.stage == 2 and k == AT["dve_norm"]:
                        norm(d)
                    for part in range(3):
                        if d.valid and d.stage == 2 and k == AT["dve_norm_out"][part]:
                            norm_out(d, part)
                    for m in range(HALVES):
                        if d.valid and d.stage == 1 and k == AT["dve_ffn_residual"][m]:
                            ffn_residual(d, m)

            run_steps(dve, step, {2: lambda: dve.wait_ge(late_in, 16 * LATE)})

        @block.scalar
        def _(act):
            def take_k(a):
                reached(act, k_mm, a, 1, 1)
                reached(act, k_lo, a, 1, 1, back=1)
                for m in range(HALVES):
                    nc.scalar.activation(kf[:, m], ps_a[:, m * TOKENS:(m + 1) * TOKENS], ACT.Identity,
                                         bias=col(a.stage, "k")[:, m:m + 1]).then_inc(k_out, 1)

            def written_before(a):
                if a.u_min >= 1:
                    before = Unit(a.n - (1 - a.p), (a.u_min - 1) // 2, 1 - a.p)
                    landed(act, img_written, before, 16 * 12)

            def part_q(a):
                reached(act, q_out, a, 2, 2)
                written_before(a)
                nc.scalar.copy(q_parts[:, 0], qf[:]).then_inc(q_hi, 1)

            def part_k(a):
                reached(act, k_out, a, 2, 2)
                nc.scalar.copy(k_parts[:, 0], kf[:]).then_inc(k_hi, 1)

            def max_hi(c):
                reached(act, m_turned, c, 1, 1)
                if c.u_min >= 1:
                    before = Unit(c.n - (1 - c.p), (c.u_min - 1) // 2, 1 - c.p)
                    landed(act, m_written, before, 32)
                nc.scalar.copy(m_parts[:, 0], ps_a[0:HEADS, 0:TOKENS]).then_inc(m_hi, 1)

            def hand_over(c):
                reached(act, pv_mm, c, GROUPS, GROUPS, back=2)
                reached(act, v_out, c, 1, 1)
                reached(act, bias_a_set, c, 1, 1)
                for t_ in range(2):
                    src = v_a[c.p][:, :, t_ * P:(t_ + 1) * P].rearrange("p m (j r) -> p m j r", r=HEAD)
                    dst = v_c[c.p][:].rearrange("p m (j t) c -> p t m j c", t=2)[:, t_, :, :, 0:HEAD]
                    out = nc.scalar.copy(dst, src)
                    if t_ == 0:
                        out.then_inc(handed_v, 1)
                    else:
                        out.then_inc(handed, 1)
                reached(act, t_mm, c, HEADS, HEADS, back=2)
                nc.scalar.copy(bias_c[c.p][:], bias_a[c.p][:].rearrange("p t q -> p (t q)")).then_inc(handed, 1)

            def exp(c, slot):
                reached(act, t_mm, c, HEADS, slot + 1)
                if slot in (0, 4):
                    reached(act, pv_mm, c, GROUPS, GROUPS - 1 + slot // 4, back=1)
                elif slot % 4 == 0:
                    reached(act, pv_mm, c, GROUPS, slot // 4 - 1)
                nc.scalar.activation(probs[:, slot // 4 % 2, slot % 4], ps_t[slot % 2][:], ACT.Exp,
                                     scale=SCALE).then_inc(exp_done, 1)

            def take_sums(c, half):
                reached(act, pv_mm, c, GROUPS, 2 * half + 2)
                if half == 0:
                    reached(act, sums_turned, c, 1, 1, back=2)
                nc.scalar.copy(sums[c.p][:, 2 * half:2 * half + 2],
                               ps_o[:].rearrange("p (g q) -> p g q", g=2)).then_inc(sums_out, 1)

            def take_ctx(d):
                reached(act, ctx_turned, d, 1, 1)
                reached(act, o_mm, d, 1, 1, back=1)
                nc.scalar.copy(ctx_feat[:], ps_d[0][:].rearrange("p (t q) -> p t q", t=HALVES)).then_inc(ctx_out, 1)

            def relu(d, m2):
                act.wait_ge(hid_mm, d.batch * 4 + (m2 + 1))
                for m in range(2):
                    nc.scalar.activation(hid[:, 2 * m2 + m], ps_d[m2 % 2][:, m * TOKENS:(m + 1) * TOKENS], ACT.Relu,
                                         bias=b1[:, 2 * m2 + m:2 * m2 + m + 1]).then_inc(relu_done, 1)

            def step(a, b, c, c_before, d):
                for k in range(HEADS):
                    if c.valid and k == AT["act_max_hi"]:
                        max_hi(c)
                    if c.valid and k == AT["act_hand_over"]:
                        hand_over(c)
                    if a.valid and k == AT["act_part_q"]:
                        part_q(a)
                    if a.valid and k == AT["act_take_k"]:
                        take_k(a)
                    if a.valid and k == AT["act_part_k"]:
                        part_k(a)
                    if k < SHIFT and c_before.valid:
                        exp(c_before, k + HEADS - SHIFT)
                    if k >= SHIFT and c.valid:
                        exp(c, k - SHIFT)
                    for half in range(2):
                        at = SHIFT + 8 * half + 4 + WEIGH_AFTER + 1
                        of = c if at < HEADS else c_before
                        if of.valid and k == at % HEADS:
                            take_sums(of, half)
                    if d.valid and k == AT["act_take_ctx"]:
                        take_ctx(d)
                    if d.valid and d.stage == 1:
                        for m2 in range(4):
                            if k == AT["act_relu"][m2]:
                                relu(d, m2)

            act.dma_start(max_sign[STACK_ROWS:P, :], t["max_sign"]).then_inc(signs_in, 16)
            act.dma_start(ident[:], t["ident"]).then_inc(signs_in, 16)
            for c in "kv":
                act.dma_start(w[0][c][:], feat(t[f"w{c}0"])).then_inc(first_in, 16)
            act.dma_start(bv[:, 0, :], t["bv0"].broadcast_to([P, WIDTH])).then_inc(first_in, 16)
            act.dma_start(w[0]["o"][:], feat(t["wo0"])).then_inc(wo_in, 16)
            act.wait_ge(signs_in, 32)
            for p in range(2):
                nc.scalar.copy(k_stack[p][STACK_ROWS:P], max_sign[STACK_ROWS:P, :, None].broadcast_to(
                    [P - STACK_ROWS, HEADS, TOKENS])).then_inc(signs_set, 1)
            act.wait_ge(const_set, 5)
            act.wait_ge(first_in, 16 * FIRST)

            def load_late():
                for s in range(1, STAGES):
                    for c in "qkvo":
                        act.dma_start(w[s][c][:], feat(t[f"w{c}{s}"])).then_inc(late_in, 16)
                act.dma_start(bv[:, 1, :], t["bv1"].broadcast_to([P, WIDTH])).then_inc(late_in, 16)
                for to, name in ((w1, "w1"), (w2, "w2")):
                    act.dma_start(to[:], feat(t[name])).then_inc(late_in, 16)
                for to, name in ((b1, "b1"), (b2, "b2")):
                    act.dma_start(to[:], t[name]).then_inc(late_in, 16)
                for to, name in ((gamma, "gamma"), (beta, "beta")):
                    act.dma_start(to[:], t[name].broadcast_to([P, WIDTH])).then_inc(late_in, 16)

            run_steps(act, step, {1: load_late, 2: lambda: act.wait_ge(late_in, 16 * LATE)})

        @block.gpsimd
        def _(pool):
            def lo_q(a):
                reached(pool, q_hi, a, 1, 1)
                nc.gpsimd.tensor_tensor(q_parts[:, 1], qf[:], q_parts[:, 0].bitcast(F32), ALU.subtract
                                        ).then_inc(q_lo, 1)

            def lo_k(a):
                reached(pool, k_hi, a, 1, 1)
                nc.gpsimd.tensor_tensor(k_parts[:, 1], kf[:], k_parts[:, 0].bitcast(F32), ALU.subtract
                                        ).then_inc(k_lo, 1)

            def rstd_of(d):
                pool.wait_ge(guess, (d.batch + 1) * 3)
                for i in range(NEWTON):
                    now, new = rstd[:, i % 2], rstd[:, (i + 1) % 2]
                    done = d.batch * NEWTON_OPS + 4 * i
                    nc.gpsimd.tensor_tensor(newton[:, 0], now, now, ALU.mult).then_inc(rstd_set, 1)
                    pool.wait_ge(rstd_set, done + 1)
                    nc.gpsimd.tensor_tensor(newton[:, 1], newton[:, 0], var_eps[:], ALU.mult).then_inc(rstd_set, 1)
                    pool.wait_ge(rstd_set, done + 2)
                    apart(pool, pool_passed)
                    nc.gpsimd.tensor_scalar(newton[:, 2], newton[:, 1], -0.5, 1.5, ALU.mult, ALU.add
                                            ).then_inc(rstd_set, 1)
                    pool.wait_ge(rstd_set, done + 3)
                    nc.gpsimd.tensor_tensor(new, newton[:, 2], now, ALU.mult).then_inc(rstd_set, 1)
                    pool.wait_ge(rstd_set, done + 4)

            def step(a, b, c, c_before, d):
                for k in range(HEADS):
                    if a.valid and k == AT["pool_lo_q"]:
                        lo_q(a)
                    if a.valid and k == AT["pool_lo_k"]:
                        lo_k(a)
                    if d.valid and d.stage == 2 and k == AT["pool_rstd"]:
                        rstd_of(d)

            nc.gpsimd.memset(k_stack[1][0:STACK_ROWS].bitcast(F32), 0.0).then_inc(k_zeroed[1], 1)
            run_steps(pool, step)


_OUT = ("out", (BATCH, TOKENS, WIDTH))


def kernel(**inputs):
    from concourse import bacc
    from concourse.bass_utils import run_bass_kernel_spmd

    a = {k: np.asarray(v) for k, v in inputs.items()}

    def columns(v):
        return v.reshape(-1, P).T

    def both(mask):
        return np.stack([np.swapaxes(mask, 1, 2), mask], axis=1)

    def words(mask):
        return np.ascontiguousarray(mask).view(np.int32)

    ins = {
        "x": np.swapaxes(a["x"], 1, 2),
        "ctx": np.swapaxes(a["ctx_1024"], 1, 2),
        "mask0": words(both(a["mask_Bx1xSxS2_bk0"][:, 0])),
        "mask1": words(both(a["mask_Bx1xSxS2_bf1"][:, 0])),
        "mask2": both(a["mask_BxSxS2_ik1"]),
        "w1": a["L0_xattn_W1"], "w2": a["L0_xattn_W2"],
        "b1": columns(a["L0_xattn_b1"]), "b2": columns(a["L0_xattn_b2"]),
        "bv0": a["L0_xattn_sbv"][None], "bv1": a["L0_xattn_cbv"][None],
        "gamma": a["L1_xattn_gamma"][None], "beta": a["L1_xattn_beta"][None],
        "cols": np.concatenate([columns(a[f"L0_xattn_{s}b{c}"]) for s in "sc" for c in "qko"], axis=1),
        "ident": np.eye(P, dtype=np.float32),
    }
    sign = np.zeros((P - STACK_ROWS, HEADS), np.float32)
    sign[0:2, 0:PAIRS] = -1.0
    sign[2:4, PAIRS:HEADS] = -1.0
    ins["max_sign"] = sign
    for c in "qkvo":
        ins[f"w{c}0"] = a[f"L0_xattn_sW{c}"]
        ins[f"w{c}1"] = a[f"L0_xattn_cW{c}"]
        ins[f"w{c}2"] = a[f"L1_xattn_W_{c.upper()}"].T

    nc = bacc.Bacc("TRN2", target_bir_lowering=False, num_devices=1)
    arrays, tensors = {}, {}
    for name, v in ins.items():
        v = np.ascontiguousarray(v)
        arrays[f"in_{name}"] = v
        tensors[name] = nc.dram_tensor(f"in_{name}", v.shape, mybir.dt.from_np(v.dtype), kind="ExternalInput").ap()
    tensors["out"] = nc.dram_tensor("out", _OUT[1], F32, kind="ExternalOutput").ap()
    build(nc, tensors)
    return run_bass_kernel_spmd(nc, [arrays], core_ids=[0]).results[0]["out"]
```

```python
from contextlib import ExitStack

import numpy as np

import concourse.bass as bass
from concourse import mybir

P = 128
BATCH, TOKENS, WIDTH, HEADS, HIDDEN = 8, 256, 256, 16, 1024
HEAD = WIDTH // HEADS
STAGES = 3
UNITS = STAGES * BATCH
HALVES = WIDTH // P
PAIRS = HEADS // 2
PARTS = 3
HALF_ROWS = PARTS * HEAD
STACK_ROWS = 2 * HALF_ROWS
MAX_ROWS = STACK_ROWS + 4
IMG_WRITES = 16 * 2 * PARTS
STACK_READS = 16 * 4
STACK_PARTS = ((0, 2), (2, 5), (5, 8))
GROUPS = 4
SHIFT = 6
WEIGH_AFTER = 5
AT = {
    "pe_turn_sums": 0, "dve_normalise": (0, 1), "pe_turn_ctx": 2, "act_take_ctx": 3, "pe_project_out": 5,
    "dve_residual": 6, "dve_norm": 5, "pool_rstd": 13, "dve_norm_out": (13, 14, 15), "pe_hidden": (10, 10, 11, 12),
    "act_relu": (9, 9, 11, 11), "pe_ffn_out": (13, 13, 14, 14), "dve_ffn_residual": (13, 14), "pe_turn_max": 2,
    "act_max_hi": 1, "dve_max_lo": 2, "act_hand_over": 4, "dve_allow": 12, "pe_count": 3, "dve_masks": (3, 4, 6),
    "pe_q": 4, "dve_take_q": 4, "act_part_q": 5, "pool_lo_q": 8, "pe_k": 6, "act_take_k": 6, "act_part_k": 7,
    "pool_lo_k": 8, "pe_v": 10, "dve_take_v": 10, "act_x_hi": 0, "pool_x_lo": 0,
}
SCALE = HEAD ** -0.5
BIG = 1.0e30
HUGE = 3.0e38
EPS = 1e-5
NEWTON = 3
NEWTON_OPS = 4 * NEWTON

F32 = mybir.dt.float32
F32R = mybir.dt.float32r
BF16 = mybir.dt.bfloat16
U8 = mybir.dt.uint8
I32 = mybir.dt.int32
ALU = mybir.AluOpType
ACT = mybir.ActivationFunctionType


class Unit:

    def __init__(self, n, n_min, p):
        self.n, self.p = n, p
        self.u = n * 2 + p
        self.u_min = 2 * n_min + p
        self.stage = self.u_min // BATCH
        self.valid = 0 <= self.u_min < UNITS
        self.batch = self.u - BATCH * self.stage


def reached(eng, sem, unit, per, count, back=0):
    least = per * (unit.u_min - back) + count
    if unit.u_min - back >= 0 and least > 0:
        eng.wait_ge(sem, unit.u * per + (count - per * back))


def landed(eng, sem, unit, per, back=0):
    if unit.u_min - 2 * back >= 0:
        eng.wait_ge(sem[unit.p], (unit.n - back + 1) * per)


def apart(eng, sem):
    eng.sem_inc(sem, 1)


AHEAD = (2, 1, 0, -1, -2)


def steps(aheads):
    def work(i):
        out = []
        for par in range(2):
            for ahead in aheads:
                u = 2 * i + par + ahead
                has_stage = ahead in (3, 2, -2) and 0 <= u < UNITS
                out.append((u // BATCH if has_stage else 0 <= u < UNITS, u >= 2))
        return out

    runs = []
    for i in range(-1, UNITS // 2 + 1):
        if runs and work(i) == work(runs[-1][0]):
            runs[-1][1] = i + 1
        else:
            runs.append([i, i + 1])
    return runs


def run_steps(eng, body, before=None, aheads=AHEAD):
    for run, (first, end) in enumerate(steps(aheads)):
        if before and run in before:
            before[run]()

        def two_steps(i):
            for par in range(2):
                def at(ahead):
                    o = par + ahead
                    return Unit(i + o // 2, first + o // 2, o % 2)
                body(*[at(ahead) for ahead in aheads])
        if end - first == 1:
            two_steps(first)
        else:
            with eng.Fori(first, end) as i:
                two_steps(i)


def head_of(slot):
    return slot // 2 + (slot % 2) * PAIRS


def build(nc, t):
    ctx = ExitStack()
    with ctx:
        def sb(name, shape, dt=F32):
            return ctx.enter_context(nc.sbuf_tensor(name, shape, dt))

        def sem(name):
            return ctx.enter_context(nc.semaphore(name))

        def sem2(name):
            return [sem(f"{name}{p}") for p in range(2)]

        def two(name, shape, dt=F32):
            return [sb(f"{name}{p}", shape, dt) for p in range(2)]

        w = [{c: sb(f"w{c}{s}", [P, 2, HALVES, WIDTH], F32R) for c in "qkv"} for s in range(STAGES)]
        wo = [sb(f"wo{s}", [P, HALVES, WIDTH]) for s in range(STAGES)]
        w1 = sb("w1", [P, HALVES, HIDDEN])
        w2 = sb("w2", [P, HIDDEN // P, WIDTH])
        cols = sb("cols", [P, 2 * 3 * HALVES])
        zero_col = sb("zero_col", [P, HALVES])
        b1 = sb("b1", [P, HIDDEN // P])
        b2 = sb("b2", [P, HALVES])
        bv = sb("bv", [P, STAGES - 1, WIDTH])
        gamma = sb("gamma", [P, WIDTH])
        beta = sb("beta", [P, WIDTH])
        ident = sb("ident", [P, P])
        ones = sb("ones", [P, P], BF16)
        max_sign = sb("max_sign", [P, HEADS])
        xq = two("xq", [P, HALVES, TOKENS])
        xkv = two("xkv", [P, HALVES, TOKENS])
        xq_parts = sb("xq_parts", [P, 2, HALVES, TOKENS], F32R)
        xkv_parts = sb("xkv_parts", [P, 2, HALVES, TOKENS], F32R)
        raw32 = sb("raw32", [P, 2, HALVES, TOKENS], I32)
        raw_words = raw32[:, :, :, 0:TOKENS // 4]
        raw8 = raw32[:].bitcast(U8)[:, :, :, 0:TOKENS]
        allow = sb("allow", [P, 2, HALVES, TOKENS], BF16)
        some = sb("some", [P, TOKENS], BF16)
        none = sb("none", [P, TOKENS], BF16)
        some_big = sb("some_big", [P, HALVES])
        bias = two("bias", [P, HALVES, TOKENS], BF16)
        ident16 = sb("ident16", [P, P], BF16)
        bias_a = two("bias_a", [P, HALVES, TOKENS], BF16)
        v_a = two("v_a", [P, HALVES, WIDTH])
        qf = sb("qf", [P, HALVES, TOKENS])
        kf = sb("kf", [P, HALVES, TOKENS])
        q_parts = sb("q_parts", [P, 2, HALVES, TOKENS], F32R)
        k_parts = sb("k_parts", [P, 2, HALVES, TOKENS], F32R)
        q_stack = two("q_stack", [P, PAIRS, TOKENS], F32R)
        k_stack = two("k_stack", [P, HEADS, TOKENS], F32R)
        mx = two("mx", [P, HALVES, HEADS])
        m_parts = sb("m_parts", [HEADS, 2, TOKENS], F32R)
        probs = sb("probs", [P, 2, 4, HALVES * TOKENS])
        bias_c = two("bias_c", [P, HALVES * TOKENS], BF16)
        v_c = two("v_c", [P, HALVES, HEADS, 32])
        sums = two("sums", [P, GROUPS, TOKENS])
        rcp = sb("rcp", [P, HALVES, HEADS])
        res = two("res", [P, HALVES, TOKENS])
        hid = sb("hid", [P, HIDDEN // P, TOKENS])
        ctx_tok = hid[:, 0:HALVES]
        ctx_feat = hid[:, HALVES:2 * HALVES]
        stats = sb("stats", [P, HALVES, 6])
        aggr = sb("aggr", [P, HALVES, 2])
        var_eps = sb("var_eps", [P, HALVES])
        guess_bits = sb("guess_bits", [P, HALVES], I32)
        rstd = sb("rstd", [P, 2, HALVES])
        newton = sb("newton", [P, 3, HALVES])

        def bank(name):
            return ctx.enter_context(nc.psum_tensor(name, [P, 512], F32))

        ps_a = bank("ps_a")
        ps_s = [bank(f"ps_s{i}") for i in range(2)]
        ps_t = [bank(f"ps_t{i}") for i in range(2)]
        ps_o = bank("ps_o")
        ps_d = [bank(f"ps_d{i}") for i in range(2)]

        x_wait = nc.dram_tensor("x_wait", [UNITS, WIDTH, TOKENS], F32).ap()
        q_img = nc.dram_tensor("q_img", [2, PARTS, HEAD, PAIRS, HALVES, TOKENS], F32).ap()
        k_img = nc.dram_tensor("k_img", [2, PARTS, HEAD, PAIRS, HALVES, TOKENS], F32).ap()
        m_img = nc.dram_tensor("m_img", [2, 2, 2, PAIRS, TOKENS], F32).ap()

        first_in, signs_in, wo_in = sem("first_in"), sem("signs_in"), sem("wo_in")
        late_in, ffn_in = sem("late_in"), sem("ffn_in")
        w_hi, w_lo_first, w_lo, x_hi, x_lo = sem("w_hi"), sem("w_lo_first"), sem("w_lo"), sem("x_hi"), sem("x_lo")
        const_set, signs_set, k_zeroed = sem("const_set"), sem("signs_set"), sem2("k_zeroed")
        in_ready, mask_ready = sem2("in_ready"), sem2("mask_ready")
        img_written = sem2("img_written")
        stack_ready = [sem2(f"stack_ready_{g}_") for g in range(len(STACK_PARTS))]
        m_written, m_ready = sem2("m_written"), sem2("m_ready")
        res_ready, stored = sem2("res_ready"), sem2("stored")
        count_mm, q_mm, k_mm, v_mm = sem("count_mm"), sem("q_mm"), sem("k_mm"), sem("v_mm")
        m_turned, s_mm, t_mm, pv_mm = sem("m_turned"), sem("s_mm"), sem("t_mm"), sem("pv_mm")
        sums_turned, ctx_turned, o_mm = sem("sums_turned"), sem("ctx_turned"), sem("o_mm")
        hid_mm, ffn_mm = sem("hid_mm"), sem("ffn_mm")
        allow_set, some_set, none_set, big_set = sem("allow_set"), sem("some_set"), sem("none_set"), sem("big_set")
        bias_a_set, bias_set, q_out, v_out = sem("bias_a_set"), sem("bias_set"), sem("q_out"), sem("v_out")
        max_set, m_lo, rcp_set, normed = sem("max_set"), sem("m_lo"), sem("rcp_set"), sem("normed")
        y_set, d_half_done, handed_v = sem("y_set"), sem("d_half_done"), sem("handed_v")
        d_done, ln_stats, ln_aggr, ln_gamma, ln_out = (
            sem("d_done"), sem("ln_stats"), sem("ln_aggr"), sem("ln_gamma"), sem("ln_out"))
        k_out, q_hi, k_hi, m_hi, exp_done = sem("k_out"), sem("q_hi"), sem("k_hi"), sem("m_hi"), sem("exp_done")
        sums_out, ctx_out, handed, relu_done = sem("sums_out"), sem("ctx_out"), sem("handed"), sem("relu_done")
        q_lo, k_lo, rstd_set = sem("q_lo"), sem("k_lo"), sem("rstd_set")
        dve_passed, pool_passed, sp_passed = sem("dve_passed"), sem("pool_passed"), sem("sp_passed")
        guess, seen_set = sem("guess"), sem("seen_set")

        FIRST, LATE = 5, 4 * (STAGES - 1) + 2 + 1 + 2

        def col(stage, which):
            if stage == 2:
                return zero_col
            o = (3 * stage + "qko".index(which)) * HALVES
            return cols[:, o:o + HALVES]

        def landing(s, c):
            i = "qkv".index(c)
            if s == 0:
                return probs[:, 0, i].rearrange("p (t e) -> p t e", t=HALVES)
            if s == 1:
                return w1[:].rearrange("p t (n e) -> p (t n) e", e=WIDTH)[:, HALVES * i:HALVES * (i + 1)]
            return w2[:, HALVES * i:HALVES * (i + 1)]

        def feat(ap):
            return ap.rearrange("(t p) q -> p t q", p=P)

        block = ctx.enter_context(nc.Block())

        @block.sync
        def _(sp):
            sp.dma_start(landing(0, "q"), feat(t["wq0"])).then_inc(first_in, 16)
            sp.dma_start(cols[:], t["cols"]).then_inc(first_in, 16)

            def load(a):
                reached(sp, x_lo, a, 2, 2, back=2)
                apart(sp, sp_passed)
                x_in = t["x"][a.batch] if a.stage == 0 else x_wait[a.u]
                if a.stage > 0:
                    landed(sp, stored, a, 16, back=BATCH // 2)
                    apart(sp, sp_passed)
                if a.stage == 0:
                    for t_ in range(HALVES):
                        sp.dma_start(xq[a.p][:, t_], x_in[t_ * P:(t_ + 1) * P]).then_inc(in_ready[a.p], 16)
                else:
                    sp.dma_start(xq[a.p][:], feat(x_in)).then_inc(in_ready[a.p], 16)
                    sp.dma_start(xkv[a.p][:], feat(t["ctx"][a.batch])).then_inc(in_ready[a.p], 16)

            def load_mask(a):
                reached(sp, allow_set, a, 2, 2, back=1)
                apart(sp, sp_passed)
                raw = raw32 if a.stage == 2 else raw_words
                for o in range(2):
                    sp.dma_start(raw[:, o], t[f"mask{a.stage}"][a.batch, o].rearrange("(t p) q -> p t q", p=P)
                                 ).then_inc(mask_ready[a.p], 16)

            def write_stacks(a):
                for ready in stack_ready:
                    landed(sp, ready, a, STACK_READS, back=1)
                    apart(sp, sp_passed)
                for parts, img, part, places, done in ((q_parts, q_img, 0, (0, 1), q_hi), (q_parts, q_img, 1, (2,), q_lo),
                                                       (k_parts, k_img, 0, (0, 2), k_hi), (k_parts, k_img, 1, (1,), k_lo)):
                    reached(sp, done, a, 1, 1)
                    apart(sp, sp_passed)
                    for c in places:
                        sp.dma_start(img[a.p, c].rearrange("r j t q -> j r (t q)"),
                                     parts[:, part].bitcast(F32).rearrange("p t q -> p (t q)")
                                     ).then_inc(img_written[a.p], 16)

            def read_stacks(a, g):
                landed(sp, img_written, a, IMG_WRITES)
                apart(sp, sp_passed)
                if a.u_min < 2 and g == 0:
                    sp.wait_ge(k_zeroed[a.p], 1)
                first, end = STACK_PARTS[g]
                reached(sp, t_mm, a, HEADS, 2 * end, back=2)
                apart(sp, sp_passed)
                j = slice(first, end)
                sem_ = stack_ready[g][a.p]
                for half in range(2):
                    rows = slice(half * HALF_ROWS, (half + 1) * HALF_ROWS)
                    heads = slice(half * PAIRS + first, half * PAIRS + end)
                    for stack, img in ((k_stack[a.p][rows, heads, :], k_img), (q_stack[a.p][rows, j, :], q_img)):
                        sp.dma_start(stack.bitcast(F32), img[a.p][:, :, j, half, :].rearrange("c r j q -> (c r) j q")
                                     ).then_inc(sem_, 16)

            def pass_max(c):
                landed(sp, m_ready, c, 16, back=1)
                apart(sp, sp_passed)
                reached(sp, m_lo, c, 1, 1)
                apart(sp, sp_passed)
                for half in range(2):
                    sp.dma_start(m_img[c.p, half].rearrange("c j q -> j c q"),
                                 m_parts[half * PAIRS:(half + 1) * PAIRS].bitcast(F32)).then_inc(m_written[c.p], 16)
                landed(sp, m_written, c, 32)
                apart(sp, sp_passed)
                reached(sp, t_mm, c, HEADS, HEADS, back=2)
                apart(sp, sp_passed)
                sp.dma_start(q_stack[c.p][STACK_ROWS:MAX_ROWS].bitcast(F32),
                             m_img[c.p].rearrange("t c j q -> (t c) j q")).then_inc(m_ready[c.p], 16)

            def load_res(d):
                landed(sp, stored, d, 16, back=1)
                apart(sp, sp_passed)
                x_in = t["x"][d.batch] if d.stage == 0 else x_wait[d.u]
                sp.dma_start(res[d.p][:], feat(x_in)).then_inc(res_ready[d.p], 16)

            def store(d):
                if d.stage == 2:
                    eng_out = t["out"][d.batch].rearrange("(t p) e -> p t e", p=P)
                    sp.wait_ge(ln_out, d.batch + 1)
                    apart(sp, sp_passed)
                    sp.dma_start(eng_out, res[d.p][:]).then_inc(stored[d.p], 16)
                else:
                    reached(sp, d_done, d, 1, 1)
                    apart(sp, sp_passed)
                    sp.dma_start(feat(x_wait[d.u + BATCH]), res[d.p][:]
                                 ).then_inc(stored[d.p], 16)

            def step(a_next, a, b, c, c_before, d):
                if b.valid:
                    read_stacks(b, 1)
                if a_next.valid and a_next.u_min >= 2:
                    load(a_next)
                if d.valid:
                    load_res(d)
                if c.valid:
                    pass_max(c)
                if a_next.valid:
                    load_mask(a_next)
                if b.valid:
                    read_stacks(b, 2)
                if a.valid:
                    write_stacks(a)
                    read_stacks(a, 0)
                if d.valid:
                    store(d)

            def load_first():
                load(Unit(0, 0, 0))
                load_mask(Unit(0, 0, 0))
                load(Unit(0, 0, 1))

            run_steps(sp, step, {0: load_first}, (3,) + AHEAD)
            for p in range(2):
                sp.wait_ge(stored[p], 16 * UNITS // 2)

        @block.tensor
        def _(pe):
            mm = nc.tensor.matmul

            def count_keys(a):
                reached(pe, allow_set, a, 2, 1)
                reached(pe, some_set, a, 1, 1, back=1)
                reached(pe, big_set, a, 1, 1, back=1)
                reached(pe, normed, a, 2, 2, back=4)
                for k in range(HALVES):
                    mm(ps_d[1][:, 0:TOKENS], ones[:], allow[:, 0, k, :], start=(k == 0), stop=(k == HALVES - 1))
                for q in range(HALVES):
                    for k in range(HALVES):
                        last = mm(ps_d[1][:, TOKENS + 2 * q:TOKENS + 2 * q + 2], allow[:, 0, k, q * P:(q + 1) * P],
                                  ones[:, 0:2], start=(k == 0), stop=(k == HALVES - 1))
                last.then_inc(count_mm, 1)

            passes = [(k, left, right) for left, right in ((0, 0), (0, 1), (1, 0)) for k in range(HALVES)]

            def project(stationary, moving, done):
                for m in range(HALVES):
                    for i, (k, left, right) in enumerate(passes):
                        last = mm(ps_a[:, m * TOKENS:(m + 1) * TOKENS], stationary[:, left, k, m * P:(m + 1) * P],
                                  moving[:, right, k, :], start=(i == 0), stop=(i == len(passes) - 1))
                last.then_inc(done, 1)

            def project_q(a):
                if a.u_min == 0:
                    pe.wait_ge(w_lo_first, 1)
                reached(pe, x_lo, a, 2, 2)
                reached(pe, v_out, a, 1, 1, back=1)
                reached(pe, m_lo, a, 1, 1, back=2)
                project(w[a.stage]["q"], xq_parts, q_mm)

            def project_k(a):
                if a.u_min == 0:
                    pe.wait_ge(w_lo_first, 2)
                reached(pe, q_out, a, 2, 2)
                project(w[a.stage]["k"], xkv_parts if a.stage else xq_parts, k_mm)

            def project_v(a):
                if a.u_min == 0:
                    pe.wait_ge(w_lo_first, 3)
                reached(pe, k_out, a, 2, 2)
                project(xkv_parts if a.stage else xq_parts, w[a.stage]["v"], v_mm)

            def scores(b, slot):
                for g, (first, _) in enumerate(STACK_PARTS):
                    if slot == 2 * first:
                        landed(pe, stack_ready[g], b, STACK_READS)
                reached(pe, max_set, b, 2 * HEADS, 2 * slot - 2)
                if slot < 2:
                    reached(pe, max_set, b, 2 * HEADS, 2 * HEADS + 2 * slot - 2, back=1)
                for q in range(HALVES):
                    last = mm(ps_s[slot % 2][:, q * TOKENS:(q + 1) * TOKENS],
                              q_stack[b.p][0:STACK_ROWS, slot // 2, q * P:(q + 1) * P],
                              k_stack[b.p][0:STACK_ROWS, head_of(slot), :], start=True, stop=True)
                last.then_inc(s_mm, 1)

            def turn_max(c):
                if c.u_min == 0:
                    pe.wait_ge(signs_in, 32)
                reached(pe, max_set, c, 2 * HEADS, 2 * HEADS)
                reached(pe, v_out, c, 1, 1)
                if c.u_min + 1 < UNITS:
                    reached(pe, v_out, c, 1, 2)
                for q in range(HALVES):
                    last = nc.tensor.transpose(ps_a[0:HEADS, q * P:(q + 1) * P], mx[c.p][:, q, :], ident[:])
                last.then_inc(m_turned, 1)

            def scores_less_max(c, slot):
                if slot == 0:
                    if c.u_min == 0:
                        pe.wait_ge(signs_set, 3)
                    landed(pe, m_ready, c, 16)
                    reached(pe, handed, c, 2, 2)
                reached(pe, exp_done, c, HEADS, slot - 1)
                if slot < 1:
                    reached(pe, exp_done, c, HEADS, HEADS + slot - 1, back=1)
                mm(ps_t[slot % 2][:], ident16[:], bias_c[c.p][:], start=True, stop=False, skip_group_check=True)
                for k in range(HALVES):
                    last = mm(ps_t[slot % 2][:, k * TOKENS:(k + 1) * TOKENS],
                              k_stack[c.p][0:MAX_ROWS, head_of(slot), k * P:(k + 1) * P],
                              q_stack[c.p][0:MAX_ROWS, slot // 2, :], start=False, stop=(k == HALVES - 1),
                              skip_group_check=True)
                last.then_inc(t_mm, 1)

            def weigh_values(c, g):
                reached(pe, exp_done, c, HEADS, 4 * g + 4)
                if g == 0:
                    reached(pe, handed, c, 2, 2)
                if g % 2 == 0:
                    reached(pe, sums_out, c, 2, g // 2)
                for k in range(HALVES):
                    for j in range(4):
                        last = mm(ps_o[32 * j:32 * j + 32, (g % 2) * TOKENS:(g % 2 + 1) * TOKENS],
                                  v_c[c.p][:, k, 4 * g + j, :], probs[:, g % 2, j, k * TOKENS:(k + 1) * TOKENS],
                                  start=(k == 0), stop=(k == HALVES - 1), tile_position=(0, 32 * j))
                last.then_inc(pv_mm, 1)

            def turn_sums(d):
                reached(pe, sums_out, d, 2, 2)
                reached(pe, d_done, d, 1, 1, back=1)
                for q in range(HALVES):
                    for g in range(GROUPS):
                        last = nc.tensor.transpose(ps_d[q][:, g * P:(g + 1) * P],
                                                   sums[d.p][:, g, q * P:(q + 1) * P], ident[:])
                last.then_inc(sums_turned, 1)

            def turn_ctx(d):
                reached(pe, normed, d, 2, 2)
                for f in range(HALVES):
                    for q in range(HALVES):
                        last = nc.tensor.transpose(ps_d[0][:, f * TOKENS + q * P:f * TOKENS + (q + 1) * P],
                                                   ctx_tok[:, q, f * P:(f + 1) * P], ident[:])
                last.then_inc(ctx_turned, 1)

            def project_out(d):
                reached(pe, ctx_out, d, 1, 1)
                if d.u_min + 4 < UNITS:
                    reached(pe, some_set, d, 1, 5)
                    reached(pe, big_set, d, 1, 5)
                w_out = wo[d.stage]
                if d.stage < 2:
                    for m in range(HALVES):
                        for k in range(HALVES):
                            last = mm(ps_d[1][:, m * TOKENS:(m + 1) * TOKENS], w_out[:, k, m * P:(m + 1) * P],
                                      ctx_feat[:, k, :], start=(k == 0), stop=(k == HALVES - 1))
                else:
                    landed(pe, res_ready, d, 16)
                    for m in range(HALVES):
                        for k in range(HALVES):
                            mm(ps_d[1][:, m * WIDTH:(m + 1) * WIDTH], ctx_feat[:, k, m * P:(m + 1) * P],
                               w_out[:, k, :], start=(k == 0), stop=False, skip_group_check=True)
                        for k in range(HALVES):
                            last = mm(ps_d[1][:, m * WIDTH + k * P:m * WIDTH + (k + 1) * P],
                                      res[d.p][:, k, m * P:(m + 1) * P], ident[:], start=False,
                                      stop=(k == HALVES - 1), skip_group_check=True)
                last.then_inc(o_mm, 1)

            def hidden(d, m2):
                if m2 == 0 and d.u_min == BATCH:
                    pe.wait_ge(ffn_in, 32)
                if m2 == 0:
                    pe.wait_ge(y_set, (d.batch + 1) * 2)
                elif m2 > 1:
                    pe.wait_ge(relu_done, d.batch * 8 + 2 * (m2 - 1))
                for m in range(2):
                    for k in range(HALVES):
                        o = (2 * m2 + m) * P
                        last = mm(ps_d[m2 % 2][:, m * TOKENS:(m + 1) * TOKENS], w1[:, k, o:o + P],
                                  res[d.p][:, k, :], start=(k == 0), stop=(k == HALVES - 1))
                last.then_inc(hid_mm, 1)

            def ffn_out(d, piece):
                m, part = divmod(piece, 2)
                if piece == 0:
                    pe.wait_ge(relu_done, (d.batch + 1) * 8)
                for k in range(4 * part, 4 * part + 4):
                    last = mm(ps_d[m][:, 0:TOKENS], w2[:, k, m * P:(m + 1) * P],
                              hid[:, k, :], start=(k == 0), stop=(k == HIDDEN // P - 1))
                if part == 1:
                    last.then_inc(ffn_mm, 1)

            def step(a, b, c, c_before, d):
                for k in range(HEADS):
                    if d.valid and k == AT["pe_turn_sums"]:
                        turn_sums(d)
                    if c.valid and k == AT["pe_turn_max"]:
                        turn_max(c)
                    if a.valid and k == AT["pe_count"]:
                        count_keys(a)
                    if a.valid and k == AT["pe_q"]:
                        project_q(a)
                    if a.valid and k == AT["pe_k"]:
                        project_k(a)
                    if a.valid and k == AT["pe_v"]:
                        project_v(a)
                    if b.valid:
                        scores(b, k)
                    if k < SHIFT and c_before.valid:
                        scores_less_max(c_before, k + HEADS - SHIFT)
                    if k >= SHIFT and c.valid:
                        scores_less_max(c, k - SHIFT)
                    for g in range(GROUPS):
                        at = SHIFT + 4 * g + WEIGH_AFTER
                        of = c if at < HEADS else c_before
                        if of.valid and k == at % HEADS:
                            weigh_values(of, g)
                    if d.valid and k == AT["pe_turn_ctx"]:
                        turn_ctx(d)
                    if d.valid and k == AT["pe_project_out"]:
                        project_out(d)
                    if d.valid and d.stage == 1:
                        for m2 in range(4):
                            if k == AT["pe_hidden"][m2]:
                                hidden(d, m2)
                        for piece in range(4):
                            if k == AT["pe_ffn_out"][piece]:
                                ffn_out(d, piece)

            def all_of_late():
                pe.wait_ge(late_in, 16 * LATE)
                pe.wait_ge(w_lo, 3 * (STAGES - 1))

            pe.wait_ge(const_set, 4)
            run_steps(pe, step, {1: lambda: pe.wait_ge(wo_in, 16), 4: all_of_late})

        @block.vector
        def _(dve):
            nc.vector.memset(zero_col[:], 0.0).then_inc(const_set, 1)
            nc.vector.memset(ones[:], 1.0).then_inc(const_set, 1)
            for p in range(2):
                nc.vector.memset(v_c[p][:, :, :, HEAD:32], 1.0).then_inc(const_set, 1)
            nc.vector.memset(k_stack[0][0:STACK_ROWS].bitcast(F32), 0.0).then_inc(k_zeroed[0], 1)
            dve.wait_ge(signs_in, 32)
            nc.vector.tensor_copy(ident16[:], ident[:]).then_inc(signs_set, 1)
            dve.wait_ge(const_set, 4)

            def set_allow(a):
                landed(dve, mask_ready, a, 32)
                reached(dve, count_mm, a, 1, 1, back=1)
                reached(dve, bias_a_set, a, 1, 1, back=1)
                reached(dve, bias_set, a, 2, 2, back=1)
                raw, blocked = (raw32, 1.0) if a.stage == 2 else (raw8, 0.0)
                for o in range(2):
                    nc.vector.tensor_scalar(allow[:, o], raw[:, o], blocked, None,
                                            ALU.not_equal).then_inc(allow_set, 1)

            def set_some(a):
                reached(dve, count_mm, a, 1, 1)
                reached(dve, q_out, a, 2, 2, back=1)
                reached(dve, bias_a_set, a, 1, 1, back=1)
                nc.vector.tensor_scalar(some[:], ps_d[1][:, 0:TOKENS], 1.0, None, ALU.min).then_inc(some_set, 1)
                nc.vector.tensor_scalar(
                    some_big[:], ps_d[1][:, TOKENS:TOKENS + 4].rearrange("p (q two) -> p q two", two=2)[:, :, 0],
                    1.0, BIG, ALU.min, ALU.mult).then_inc(big_set, 1)

            def set_bias(a):
                reached(dve, some_set, a, 1, 1)
                nc.vector.tensor_scalar(none[:], some[:], -1.0, 1.0, ALU.mult, ALU.add).then_inc(none_set, 1)
                reached(dve, big_set, a, 1, 1)
                reached(dve, allow_set, a, 2, 2)
                reached(dve, max_set, a, 2 * HEADS, 2 * HEADS, back=2)
                for q in range(HALVES):
                    nc.vector.tensor_scalar(bias[a.p][:, q], allow[:, 1, q], some_big[:, q:q + 1],
                                            some_big[:, q:q + 1], ALU.mult, ALU.subtract).then_inc(bias_set, 1)

            def set_bias_a(a):
                reached(dve, none_set, a, 1, 1)
                reached(dve, handed, a, 2, 2, back=2)
                nc.vector.tensor_tensor(bias_a[a.p][:], allow[:, 0], none[:, None, :].broadcast_to([P, HALVES, TOKENS]),
                                        ALU.max).then_inc(seen_set, 1)
                reached(dve, seen_set, a, 1, 1)
                nc.vector.tensor_scalar(bias_a[a.p][:], bias_a[a.p][:], BIG, -BIG, ALU.mult, ALU.add
                                        ).then_inc(bias_a_set, 1)

            def take_q(a):
                reached(dve, q_mm, a, 1, 1)
                reached(dve, q_lo, a, 1, 1, back=1)
                for m in range(HALVES):
                    nc.vector.scalar_tensor_tensor(out=qf[:, m], in0=ps_a[:, m * TOKENS:(m + 1) * TOKENS],
                                                   scalar=col(a.stage, "q")[:, m:m + 1], in1=some[:],
                                                   op0=ALU.add, op1=ALU.mult).then_inc(q_out, 1)

            def take_v(a):
                reached(dve, v_mm, a, 1, 1)
                reached(dve, handed, a, 2, 2, back=2)
                values = ps_a[:].rearrange("p (m e) -> p m e", m=HALVES)
                if a.stage == 2:
                    nc.vector.tensor_copy(v_a[a.p][:], values).then_inc(v_out, 1)
                else:
                    nc.vector.tensor_tensor(v_a[a.p][:], values,
                                            bv[:, a.stage:a.stage + 1, :].broadcast_to([P, HALVES, WIDTH]),
                                            ALU.add).then_inc(v_out, 1)

            def row_max(b, slot):
                reached(dve, s_mm, b, HEADS, slot + 1)
                if slot == 0:
                    reached(dve, bias_set, b, 2, 2)
                    reached(dve, m_turned, b, 1, 1, back=2)
                h = head_of(slot)
                apart(dve, dve_passed)
                for q in range(HALVES):
                    at = ps_s[slot % 2][:, q * TOKENS:(q + 1) * TOKENS]
                    nc.vector.tensor_tensor_reduce(at, at, bias[b.p][:, q], 1.0, -HUGE, ALU.add, ALU.max,
                                                   mx[b.p][:, q, h:h + 1]).then_inc(max_set, 1)

            def max_lo(c):
                reached(dve, m_hi, c, 1, 1)
                nc.vector.tensor_tensor(m_parts[:, 1], ps_a[0:HEADS, 0:TOKENS], m_parts[:, 0].bitcast(F32),
                                        ALU.subtract).then_inc(m_lo, 1)

            def normalise(d, q):
                reached(dve, sums_turned, d, 1, 1)
                reached(dve, normed, d, 2, 2, back=1)
                nc.vector.reciprocal(rcp[:, q], ps_d[q][:].rearrange("p (s c) -> p s c", c=32)[:, :, HEAD]
                                     ).then_inc(rcp_set, 1)
                reached(dve, ctx_turned, d, 1, 1, back=1)
                reached(dve, rcp_set, d, 2, q + 1)
                of = ps_d[q][:].rearrange("p (j t c) -> p j t c", t=2, c=32)
                to = ctx_tok[:, q].rearrange("p (t j r) -> p j t r", t=2, r=HEAD)
                by = rcp[:, q].rearrange("p (j t) -> p j t", t=2)
                nc.vector.tensor_tensor(to, of[:, :, :, 0:HEAD], by[:, :, :, None].broadcast_to([P, PAIRS, 2, HEAD]),
                                        ALU.mult).then_inc(normed, 1)

            def residual(d):
                reached(dve, o_mm, d, 1, 1)
                landed(dve, res_ready, d, 16)
                for m in range(HALVES):
                    out = nc.vector.scalar_tensor_tensor(out=res[d.p][:, m], in0=ps_d[1][:, m * TOKENS:(m + 1) * TOKENS],
                                                         scalar=col(d.stage, "o")[:, m:m + 1], in1=res[d.p][:, m],
                                                         op0=ALU.add, op1=ALU.add)
                    if d.stage == 1:
                        out.then_inc(y_set, 1)
                    else:
                        out.then_inc(d_done if m == HALVES - 1 else d_half_done, 1)

            def ffn_residual(d, m):
                dve.wait_ge(ffn_mm, d.batch * 2 + (m + 1))
                if m == 0:
                    dve.wait_ge(y_set, (d.batch + 1) * 2)
                out = nc.vector.scalar_tensor_tensor(out=res[d.p][:, m], in0=ps_d[m][:, 0:TOKENS],
                                                     scalar=b2[:, m:m + 1], in1=res[d.p][:, m],
                                                     op0=ALU.add, op1=ALU.add)
                out.then_inc(d_done if m == HALVES - 1 else d_half_done, 1)

            def norm(d):
                reached(dve, o_mm, d, 1, 1)
                for m in range(HALVES):
                    nc.vector.bn_stats(stats[:, m], ps_d[1][:, m * WIDTH:(m + 1) * WIDTH]).then_inc(ln_stats, 1)
                for m in range(HALVES):
                    dve.wait_ge(ln_stats, d.batch * 2 + (m + 1))
                    apart(dve, dve_passed)
                    nc.vector.bn_aggr(aggr[:, m], stats[:, m]).then_inc(ln_aggr, 1)
                dve.wait_ge(ln_aggr, (d.batch + 1) * 2)
                nc.vector.tensor_scalar(var_eps[:], aggr[:, :, 1], EPS, None, ALU.add).then_inc(guess, 1)
                dve.wait_ge(guess, d.batch * 3 + 1)
                nc.vector.tensor_scalar(guess_bits[:], var_eps[:].bitcast(I32), 1, None,
                                        ALU.logical_shift_right).then_inc(guess, 1)
                dve.wait_ge(guess, d.batch * 3 + 2)
                nc.vector.tensor_scalar(rstd[:, 0].bitcast(I32), guess_bits[:], -1.0, float(0x5F3759DF),
                                        ALU.mult, ALU.add).then_inc(guess, 1)

            def norm_out(d, part):
                dve.wait_ge(rstd_set, (d.batch + 1) * NEWTON_OPS)
                if part == 0:
                    landed(dve, res_ready, d, 16)
                    for m in range(HALVES):
                        out = nc.vector.tensor_scalar(res[d.p][:, m], ps_d[1][:, m * WIDTH:(m + 1) * WIDTH],
                                                      aggr[:, m, 0:1], rstd[:, NEWTON % 2, m:m + 1],
                                                      ALU.subtract, ALU.mult)
                        out.then_inc(d_done if m == HALVES - 1 else d_half_done, 1)
                elif part == 1:
                    reached(dve, d_done, d, 1, 1)
                    reached(dve, d_half_done, d, 1, 1)
                    nc.vector.tensor_tensor(res[d.p][:], res[d.p][:],
                                            gamma[:, None, :].broadcast_to([P, HALVES, WIDTH]),
                                            ALU.mult).then_inc(ln_gamma, 1)
                else:
                    dve.wait_ge(ln_gamma, d.batch + 1)
                    nc.vector.tensor_tensor(res[d.p][:], res[d.p][:],
                                            beta[:, None, :].broadcast_to([P, HALVES, WIDTH]),
                                            ALU.add).then_inc(ln_out, 1)

            def first_allow():
                set_allow(Unit(0, 0, 0))
                for i, c in enumerate("qkv"):
                    dve.wait_ge(w_hi, i + 1)
                    nc.vector.tensor_tensor(w[0][c][:, 1], landing(0, c), w[0][c][:, 0].bitcast(F32), ALU.subtract
                                            ).then_inc(w_lo_first, 1)

            def step(a_next, a, b, c, c_before, d):
                for k in range(HEADS):
                    for q in range(HALVES):
                        if d.valid and k == AT["dve_normalise"][q]:
                            normalise(d, q)
                    if a_next.valid and k == AT["dve_allow"]:
                        set_allow(a_next)
                    if c.valid and k == AT["dve_max_lo"]:
                        max_lo(c)
                    for part, set_part in enumerate((set_some, set_bias, set_bias_a)):
                        if a.valid and k == AT["dve_masks"][part]:
                            set_part(a)
                    if a.valid and k == AT["dve_take_q"]:
                        take_q(a)
                    if a.valid and k == AT["dve_take_v"]:
                        take_v(a)
                    if b.valid:
                        row_max(b, k)
                    if d.valid and d.stage < 2 and k == AT["dve_residual"]:
                        residual(d)
                    if d.valid and d.stage == 2 and k == AT["dve_norm"]:
                        norm(d)
                    for part in range(3):
                        if d.valid and d.stage == 2 and k == AT["dve_norm_out"][part]:
                            norm_out(d, part)
                    for m in range(HALVES):
                        if d.valid and d.stage == 1 and k == AT["dve_ffn_residual"][m]:
                            ffn_residual(d, m)

            run_steps(dve, step, {0: first_allow, 3: lambda: dve.wait_ge(late_in, 16 * LATE)},
                      (3,) + AHEAD)

        @block.scalar
        def _(act):
            def take_k(a):
                reached(act, k_mm, a, 1, 1)
                reached(act, k_lo, a, 1, 1, back=1)
                for m in range(HALVES):
                    nc.scalar.activation(kf[:, m], ps_a[:, m * TOKENS:(m + 1) * TOKENS], ACT.Identity,
                                         bias=col(a.stage, "k")[:, m:m + 1]).then_inc(k_out, 1)

            def written_before(a):
                if a.u_min >= 1:
                    before = Unit(a.n - (1 - a.p), (a.u_min - 1) // 2, 1 - a.p)
                    landed(act, img_written, before, IMG_WRITES)

            def split_x(a):
                landed(act, in_ready, a, 32)
                reached(act, v_mm, a, 1, 1, back=1)
                if a.stage == 0:
                    nc.scalar.copy(xq_parts[:, 0], xq[a.p][:]).then_inc(x_hi, 2)
                else:
                    for x, parts in ((xq, xq_parts), (xkv, xkv_parts)):
                        nc.scalar.copy(parts[:, 0], x[a.p][:]).then_inc(x_hi, 1)

            def part_q(a):
                reached(act, q_out, a, 2, 2)
                written_before(a)
                nc.scalar.copy(q_parts[:, 0], qf[:]).then_inc(q_hi, 1)

            def part_k(a):
                reached(act, k_out, a, 2, 2)
                nc.scalar.copy(k_parts[:, 0], kf[:]).then_inc(k_hi, 1)

            def max_hi(c):
                reached(act, m_turned, c, 1, 1)
                if c.u_min >= 1:
                    before = Unit(c.n - (1 - c.p), (c.u_min - 1) // 2, 1 - c.p)
                    landed(act, m_written, before, 32)
                nc.scalar.copy(m_parts[:, 0], ps_a[0:HEADS, 0:TOKENS]).then_inc(m_hi, 1)

            def hand_over(c):
                reached(act, pv_mm, c, GROUPS, GROUPS, back=2)
                reached(act, v_out, c, 1, 1)
                reached(act, bias_a_set, c, 1, 1)
                for t_ in range(2):
                    src = v_a[c.p][:, :, t_ * P:(t_ + 1) * P].rearrange("p m (j r) -> p m j r", r=HEAD)
                    dst = v_c[c.p][:].rearrange("p m (j t) c -> p t m j c", t=2)[:, t_, :, :, 0:HEAD]
                    out = nc.scalar.copy(dst, src)
                    if t_ == 0:
                        out.then_inc(handed_v, 1)
                    else:
                        out.then_inc(handed, 1)
                reached(act, t_mm, c, HEADS, HEADS, back=2)
                nc.scalar.copy(bias_c[c.p][:], bias_a[c.p][:].rearrange("p t q -> p (t q)")).then_inc(handed, 1)

            def exp(c, slot):
                reached(act, t_mm, c, HEADS, slot + 1)
                if slot in (0, 4):
                    reached(act, pv_mm, c, GROUPS, GROUPS - 1 + slot // 4, back=1)
                elif slot % 4 == 0:
                    reached(act, pv_mm, c, GROUPS, slot // 4 - 1)
                nc.scalar.activation(probs[:, slot // 4 % 2, slot % 4], ps_t[slot % 2][:], ACT.Exp,
                                     scale=SCALE).then_inc(exp_done, 1)

            def take_sums(c, half):
                reached(act, pv_mm, c, GROUPS, 2 * half + 2)
                if half == 0:
                    reached(act, sums_turned, c, 1, 1, back=2)
                nc.scalar.copy(sums[c.p][:, 2 * half:2 * half + 2],
                               ps_o[:].rearrange("p (g q) -> p g q", g=2)).then_inc(sums_out, 1)

            def take_ctx(d):
                reached(act, ctx_turned, d, 1, 1)
                reached(act, o_mm, d, 1, 1, back=1)
                nc.scalar.copy(ctx_feat, ps_d[0][:].rearrange("p (t q) -> p t q", t=HALVES)).then_inc(ctx_out, 1)

            def relu(d, m2):
                act.wait_ge(hid_mm, d.batch * 4 + (m2 + 1))
                for m in range(2):
                    nc.scalar.activation(hid[:, 2 * m2 + m], ps_d[m2 % 2][:, m * TOKENS:(m + 1) * TOKENS], ACT.Relu,
                                         bias=b1[:, 2 * m2 + m:2 * m2 + m + 1]).then_inc(relu_done, 1)

            def step(a, b, c, c_before, d):
                for k in range(HEADS):
                    if c.valid and k == AT["act_max_hi"]:
                        max_hi(c)
                    if c.valid and k == AT["act_hand_over"]:
                        hand_over(c)
                    if a.valid and k == AT["act_x_hi"]:
                        split_x(a)
                    if a.valid and k == AT["act_part_q"]:
                        part_q(a)
                    if a.valid and k == AT["act_take_k"]:
                        take_k(a)
                    if a.valid and k == AT["act_part_k"]:
                        part_k(a)
                    if k < SHIFT and c_before.valid:
                        exp(c_before, k + HEADS - SHIFT)
                    if k >= SHIFT and c.valid:
                        exp(c, k - SHIFT)
                    for half in range(2):
                        at = SHIFT + 8 * half + 4 + WEIGH_AFTER + 1
                        of = c if at < HEADS else c_before
                        if of.valid and k == at % HEADS:
                            take_sums(of, half)
                    if d.valid and k == AT["act_take_ctx"]:
                        take_ctx(d)
                    if d.valid and d.stage == 1:
                        for m2 in range(4):
                            if k == AT["act_relu"][m2]:
                                relu(d, m2)
                if a.u_min == 0:
                    set_signs()

            act.dma_start(max_sign[STACK_ROWS:P, :], t["max_sign"]).then_inc(signs_in, 16)
            act.dma_start(ident[:], t["ident"]).then_inc(signs_in, 16)
            for c in "kv":
                act.dma_start(landing(0, c), feat(t[f"w{c}0"])).then_inc(first_in, 16)
            act.dma_start(bv[:, 0, :], t["bv0"].broadcast_to([P, WIDTH])).then_inc(first_in, 16)
            act.dma_start(wo[0][:], feat(t["wo0"])).then_inc(wo_in, 16)
            act.wait_ge(const_set, 4)
            act.wait_ge(first_in, 16 * FIRST)
            for c in "qkv":
                nc.scalar.copy(w[0][c][:, 0], landing(0, c)).then_inc(w_hi, 1)

            def set_signs():
                act.wait_ge(signs_in, 32)
                for p in range(2):
                    nc.scalar.copy(k_stack[p][STACK_ROWS:P], max_sign[STACK_ROWS:P, :, None].broadcast_to(
                        [P - STACK_ROWS, HEADS, TOKENS])).then_inc(signs_set, 1)

            def split_late():
                act.wait_ge(late_in, 16 * LATE)
                for s in range(1, STAGES):
                    for c in "qkv":
                        nc.scalar.copy(w[s][c][:, 0], landing(s, c)).then_inc(w_hi, 1)

            def load_ffn():
                act.wait_ge(w_lo, 3 * (STAGES - 1))
                for to, name in ((w1, "w1"), (w2, "w2")):
                    act.dma_start(to[:], feat(t[name])).then_inc(ffn_in, 16)

            run_steps(act, step, {3: split_late, 4: load_ffn})

        @block.gpsimd
        def _(pool):
            def lo_x(a):
                for i, (x, parts) in enumerate(((xq, xq_parts), (xkv, xkv_parts))[0:1 if a.stage == 0 else 2]):
                    reached(pool, x_hi, a, 2, 2 if a.stage == 0 else i + 1)
                    nc.gpsimd.tensor_tensor(parts[:, 1], x[a.p][:], parts[:, 0].bitcast(F32), ALU.subtract
                                            ).then_inc(x_lo, 2 if a.stage == 0 else 1)

            def lo_q(a):
                reached(pool, q_hi, a, 1, 1)
                nc.gpsimd.tensor_tensor(q_parts[:, 1], qf[:], q_parts[:, 0].bitcast(F32), ALU.subtract
                                        ).then_inc(q_lo, 1)

            def lo_k(a):
                reached(pool, k_hi, a, 1, 1)
                nc.gpsimd.tensor_tensor(k_parts[:, 1], kf[:], k_parts[:, 0].bitcast(F32), ALU.subtract
                                        ).then_inc(k_lo, 1)

            def rstd_of(d):
                pool.wait_ge(guess, (d.batch + 1) * 3)
                for i in range(NEWTON):
                    now, new = rstd[:, i % 2], rstd[:, (i + 1) % 2]
                    done = d.batch * NEWTON_OPS + 4 * i
                    nc.gpsimd.tensor_tensor(newton[:, 0], now, now, ALU.mult).then_inc(rstd_set, 1)
                    pool.wait_ge(rstd_set, done + 1)
                    nc.gpsimd.tensor_tensor(newton[:, 1], newton[:, 0], var_eps[:], ALU.mult).then_inc(rstd_set, 1)
                    pool.wait_ge(rstd_set, done + 2)
                    apart(pool, pool_passed)
                    nc.gpsimd.tensor_scalar(newton[:, 2], newton[:, 1], -0.5, 1.5, ALU.mult, ALU.add
                                            ).then_inc(rstd_set, 1)
                    pool.wait_ge(rstd_set, done + 3)
                    nc.gpsimd.tensor_tensor(new, newton[:, 2], now, ALU.mult).then_inc(rstd_set, 1)
                    pool.wait_ge(rstd_set, done + 4)

            def step(a, b, c, c_before, d):
                for k in range(HEADS):
                    if a.valid and k == AT["pool_x_lo"]:
                        lo_x(a)
                    if a.valid and k == AT["pool_lo_q"]:
                        lo_q(a)
                    if a.valid and k == AT["pool_lo_k"]:
                        lo_k(a)
                    if d.valid and d.stage == 2 and k == AT["pool_rstd"]:
                        rstd_of(d)

            nc.gpsimd.memset(k_stack[1][0:STACK_ROWS].bitcast(F32), 0.0).then_inc(k_zeroed[1], 1)

            def split_late():
                for i in range(3 * (STAGES - 1)):
                    s, c = 1 + i // 3, "qkv"[i % 3]
                    part = w[s][c]
                    pool.wait_ge(w_hi, 3 + i + 1)
                    nc.gpsimd.tensor_tensor(part[:, 1], landing(s, c), part[:, 0].bitcast(F32), ALU.subtract
                                            ).then_inc(w_lo, 1)

            def load_late():
                for s in range(1, STAGES):
                    for c in "qkvo":
                        to = wo[s][:] if c == "o" else landing(s, c)
                        nc.gpsimd.dma_start(to, feat(t[f"w{c}{s}"])).then_inc(late_in, 16)
                nc.gpsimd.dma_start(bv[:, 1, :], t["bv1"].broadcast_to([P, WIDTH])).then_inc(late_in, 16)
                for to, name in ((b1, "b1"), (b2, "b2")):
                    nc.gpsimd.dma_start(to[:], t[name]).then_inc(late_in, 16)
                for to, name in ((gamma, "gamma"), (beta, "beta")):
                    nc.gpsimd.dma_start(to[:], t[name].broadcast_to([P, WIDTH])).then_inc(late_in, 16)

            run_steps(pool, step, {2: load_late, 3: split_late})


_OUT = ("out", (BATCH, TOKENS, WIDTH))


def kernel(**inputs):
    from concourse import bacc
    from concourse.bass_utils import run_bass_kernel_spmd

    a = {k: np.asarray(v) for k, v in inputs.items()}

    def columns(v):
        return v.reshape(-1, P).T

    def both(mask):
        return np.stack([np.swapaxes(mask, 1, 2), mask], axis=1)

    def words(mask):
        return np.ascontiguousarray(mask).view(np.int32)

    ins = {
        "x": np.swapaxes(a["x"], 1, 2),
        "ctx": np.swapaxes(a["ctx_1024"], 1, 2),
        "mask0": words(both(a["mask_Bx1xSxS2_bk0"][:, 0])),
        "mask1": words(both(a["mask_Bx1xSxS2_bf1"][:, 0])),
        "mask2": both(a["mask_BxSxS2_ik1"]),
        "w1": a["L0_xattn_W1"], "w2": a["L0_xattn_W2"],
        "b1": columns(a["L0_xattn_b1"]), "b2": columns(a["L0_xattn_b2"]),
        "bv0": a["L0_xattn_sbv"][None], "bv1": a["L0_xattn_cbv"][None],
        "gamma": a["L1_xattn_gamma"][None], "beta": a["L1_xattn_beta"][None],
        "cols": np.concatenate([columns(a[f"L0_xattn_{s}b{c}"]) for s in "sc" for c in "qko"], axis=1),
        "ident": np.eye(P, dtype=np.float32),
    }
    sign = np.zeros((P - STACK_ROWS, HEADS), np.float32)
    sign[0:2, 0:PAIRS] = -1.0
    sign[2:4, PAIRS:HEADS] = -1.0
    ins["max_sign"] = sign
    for c in "qkvo":
        ins[f"w{c}0"] = a[f"L0_xattn_sW{c}"]
        ins[f"w{c}1"] = a[f"L0_xattn_cW{c}"]
        ins[f"w{c}2"] = a[f"L1_xattn_W_{c.upper()}"].T

    nc = bacc.Bacc("TRN2", target_bir_lowering=False, num_devices=1)
    arrays, tensors = {}, {}
    for name, v in ins.items():
        v = np.ascontiguousarray(v)
        arrays[f"in_{name}"] = v
        tensors[name] = nc.dram_tensor(f"in_{name}", v.shape, mybir.dt.from_np(v.dtype), kind="ExternalInput").ap()
    tensors["out"] = nc.dram_tensor("out", _OUT[1], F32, kind="ExternalOutput").ap()
    build(nc, tensors)
    return run_bass_kernel_spmd(nc, [arrays], core_ids=[0]).results[0]["out"]
```
